# Optimizing a Trainium2 kernel written in Bass

```python
import numpy as np
import jax
import jax.numpy as jnp

def _softmax(x, axis=-1):
    return jax.nn.softmax(x, axis=axis)

def _gelu(x):
    return jax.nn.gelu(x, approximate=True)

def _silu(x):
    return jax.nn.silu(x)

def _sigmoid(x):
    return jax.nn.sigmoid(x)

def _layernorm(x, axis=-1, eps=1e-05):
    m = jnp.mean(x, axis=axis, keepdims=True)
    v = jnp.var(x, axis=axis, keepdims=True)
    return (x - m) / jnp.sqrt(v + eps)

def _scatter_add(tgt, idx, src, axis=0):
    return tgt.at[idx].add(src)

def _segment_sum(src, seg, n):
    return jax.ops.segment_sum(src, seg, n)
kernel_name = 'mk_seq_postln_d1_jaxref_r8_bf76f9'

def setup_inputs(seed: int=0):
    np.random.seed(seed)
    _w = jnp.asarray

    def _L0_attn_setup():
        import jax, jax.numpy as jnp
        import numpy as np
        DIM = 128
        HEADS = 16
        HEAD_DIM = DIM // HEADS
        FEAT = 32
        B, N = (4, 512)

        def _elu1(x):
            return jnp.where(x > 0, x + 1.0, jnp.exp(x))
        key = jax.random.key(seed)
        k_x, k_qkv, k_proj, k_wo, k_bo = jax.random.split(key, 5)
        x = jax.random.normal(k_x, (B, N, DIM), dtype=jnp.float32)
        w_qkv = jax.random.normal(k_qkv, (DIM, 3 * DIM), dtype=jnp.float32) * (1.0 / np.sqrt(DIM))
        proj_matrix = jax.random.normal(k_proj, (HEADS, HEAD_DIM, FEAT), dtype=jnp.float32) * (1.0 / np.sqrt(HEAD_DIM))
        w_out = jax.random.normal(k_wo, (DIM, DIM), dtype=jnp.float32) * (1.0 / np.sqrt(DIM))
        b_out = jax.random.normal(k_bo, (DIM,), dtype=jnp.float32) * 0.01
        return {'x': x, 'w_qkv': w_qkv, 'proj_matrix': proj_matrix, 'w_out': w_out, 'b_out': b_out}
    _L0_attn_in = _L0_attn_setup()

    def _L0_ffn_setup():
        import jax, jax.numpy as jnp
        import numpy as np
        EPS = 1e-12

        def _l2norm(v):
            n = jnp.sqrt(jnp.sum(v * v, axis=-1, keepdims=True))
            return v / jnp.maximum(n, EPS)
        key = jax.random.key(seed)
        ks = jax.random.split(key, 6)
        B, S, D, F, E = (2, 256, 128, 512, 8)
        std = 0.02
        return {'x': jax.random.normal(ks[0], (B, S, D), jnp.float32), 'Wp': jax.random.normal(ks[1], (D, D), jnp.float32) * (1.0 / np.sqrt(D)), 'sim_matrix': jax.random.normal(ks[2], (E, D), jnp.float32) * std, 'temperature': jnp.asarray(1.0, jnp.float32), 'W1': jax.random.normal(ks[3], (E, D, F), jnp.float32) * (1.0 / np.sqrt(D)), 'b1': jnp.zeros((E, F), jnp.float32), 'W2': jax.random.normal(ks[4], (E, F, D), jnp.float32) * (1.0 / np.sqrt(F)), 'b2': jnp.zeros((E, D), jnp.float32)}
    _L0_ffn_in = _L0_ffn_setup()
    _d = {'L0_attn_x': _L0_attn_in['x'], 'L0_attn_w_qkv': _L0_attn_in['w_qkv'], 'L0_attn_proj_matrix': _L0_attn_in['proj_matrix'], 'L0_attn_w_out': _L0_attn_in['w_out'], 'L0_attn_b_out': _L0_attn_in['b_out'], 'L0_ffn_Wp': _L0_ffn_in['Wp'], 'L0_ffn_sim_matrix': _L0_ffn_in['sim_matrix'], 'L0_ffn_temperature': _L0_ffn_in['temperature'], 'L0_ffn_W1': _L0_ffn_in['W1'], 'L0_ffn_b1': _L0_ffn_in['b1'], 'L0_ffn_W2': _L0_ffn_in['W2'], 'L0_ffn_b2': _L0_ffn_in['b2']}
    _x0 = _d['L0_attn_x']
    _d['L0_attn_x'] = jax.random.normal(jax.random.fold_in(jax.random.key(seed), 1), (8, 512, 128), dtype=_x0.dtype)
    del _x0
    return _d

def reference(L0_attn_x, L0_attn_w_qkv, L0_attn_proj_matrix, L0_attn_w_out, L0_attn_b_out, L0_ffn_Wp, L0_ffn_sim_matrix, L0_ffn_temperature, L0_ffn_W1, L0_ffn_b1, L0_ffn_W2, L0_ffn_b2):

    def _L0_attn_ref(x, w_qkv, proj_matrix, w_out, b_out):
        import jax, jax.numpy as jnp
        import numpy as np
        DIM = 128
        HEADS = 16
        HEAD_DIM = DIM // HEADS
        FEAT = 32
        B, N = (4, 512)

        def _elu1(x):
            return jnp.where(x > 0, x + 1.0, jnp.exp(x))
        b, n, d = x.shape
        h, hd = (HEADS, HEAD_DIM)
        qkv = x @ w_qkv
        q, k, v = jnp.split(qkv, 3, axis=-1)
        to_heads = lambda t: t.reshape(b, n, h, hd).transpose(0, 2, 1, 3)
        q, k, v = (to_heads(q), to_heads(k), to_heads(v))
        q_proj = _elu1(jnp.einsum('bhnd,hdf->bhnf', q, proj_matrix))
        k_proj = _elu1(jnp.einsum('bhnd,hdf->bhnf', k, proj_matrix))
        kv = jnp.einsum('bhnf,bhnd->bhfd', k_proj, v)
        attn = jnp.einsum('bhnf,bhfd->bhnd', q_proj, kv)
        k_sum = k_proj.sum(axis=2)
        z = 1.0 / (jnp.einsum('bhnf,bhf->bhn', q_proj, k_sum) + 1e-08)
        attn = attn * z[..., None]
        out = attn.transpose(0, 2, 1, 3).reshape(b, n, d)
        return out @ w_out + b_out

    def _L0_ffn_ref(x, Wp, sim_matrix, temperature, W1, b1, W2, b2):
        import jax, jax.numpy as jnp
        import numpy as np
        EPS = 1e-12

        def _l2norm(v):
            n = jnp.sqrt(jnp.sum(v * v, axis=-1, keepdims=True))
            return v / jnp.maximum(n, EPS)
        E = sim_matrix.shape[0]
        top_k = 2
        proj = jnp.einsum('bsd,ed->bse', x, Wp)
        pn = _l2norm(proj)
        sn = _l2norm(sim_matrix)
        gate_scores = jnp.einsum('bsd,ed->bse', pn, sn) / temperature
        top_v, top_i = jax.lax.top_k(gate_scores, top_k)
        gate_probs = jax.nn.softmax(top_v, axis=-1)
        comb = jnp.sum(jax.nn.one_hot(top_i, E, dtype=x.dtype) * gate_probs[..., None], axis=-2)
        h = jax.nn.gelu(jnp.einsum('bsd,edf->ebsf', x, W1) + b1[:, None, None, :], approximate=False)
        eo = jnp.einsum('ebsf,efd->ebsd', h, W2) + b2[:, None, None, :]
        out = jnp.einsum('ebsd,bse->bsd', eo, comb)
        return out
    x = L0_attn_x
    x = _layernorm(x + _L0_attn_ref(x, L0_attn_w_qkv, L0_attn_proj_matrix, L0_attn_w_out, L0_attn_b_out), axis=-1)
    x = _layernorm(x + _L0_ffn_ref(x, L0_ffn_Wp, L0_ffn_sim_matrix, L0_ffn_temperature, L0_ffn_W1, L0_ffn_b1, L0_ffn_W2, L0_ffn_b2), axis=-1)
    return x

_drawn_inputs = setup_inputs


def setup_inputs(seed=0):
    import zlib

    import numpy as np

    out = dict(_drawn_inputs(seed))
    spreads = {'L0_ffn_b1': (0.0, 0.1), 'L0_ffn_b2': (0.0, 0.1)}
    factors = {}
    for name, (base, spread) in spreads.items():
        noise = np.random.default_rng([zlib.crc32(name.encode()), seed]).standard_normal(out[name].shape)
        drawn = base * np.exp(spread * noise) if base else spread * noise
        out[name] = jnp.asarray(drawn.astype(out[name].dtype))
    for name, factor in factors.items():
        out[name] = (out[name] * factor).astype(out[name].dtype)
    return out
```

```python
from contextlib import ExitStack

import concourse.bass as bass
from concourse import mybir

F32 = mybir.dt.float32
F32R = mybir.dt.float32r
U32 = mybir.dt.uint32
ALU = mybir.AluOpType
ACT = mybir.ActivationFunctionType
AX = mybir.AxisListType


def build_layer(nc, x, w_qkv, proj_matrix, w_out, b_out, wp, sim, temperature, w1, b1, w2, b2, out, comb_dram):
    SEQS, N, D = x.shape
    HEADS, HD, FEAT = proj_matrix.shape
    E, _, F = w1.shape
    P = 128
    T = N // P
    NF = HEADS * FEAT
    FC = NF // P
    HC = HEADS // FC
    VW = HD + 1
    KC = HC * VW
    CH = F // P
    SLOTS = E * CH
    UNITS = SLOTS // 2
    RING = 4
    UPB = 2
    TOP = 8
    LN_EPS, DEN_EPS, NORM_EPS = 1e-5, 1e-8, 1e-12
    HEAD = 4
    HI_ON_DVE = (3, 7, 11, 15)
    assert D == P and N == 512 and NF == 512 and UNITS % RING == 0

    with ExitStack() as ctx:
        def sb(name, shape, dt=F32):
            return ctx.enter_context(nc.sbuf_tensor(name, shape, dt))

        def sem(name):
            return ctx.enter_context(nc.semaphore(name))

        ident = sb("ident", [P, P])
        iota8 = sb("iota8", [P, T, 2, E])
        iota_i = sb("iota_i", [P, T, 2, E], mybir.dt.int32)
        head_mask = sb("head_mask", [P, HEADS])
        kv_mask = sb("kv_mask", [P, HC])
        minus_half = sb("minus_half", [P, T])
        wqkv_raw = sb("wqkv_raw", [P, 3 * D])
        proj_raw = sb("proj_raw", [P, FEAT])
        wqkT = sb("wqkT", [P, 2, P])
        wq_hi, wq_lo = sb("wq_hi", [P, NF], F32R), sb("wq_lo", [P, NF], F32R)
        wk_hi, wk_lo = sb("wk_hi", [P, NF], F32R), sb("wk_lo", [P, NF], F32R)
        wv_hi, wv_lo = sb("wv_hi", [P, D], F32R), sb("wv_lo", [P, D], F32R)
        wo = sb("wo", [P, D])
        bo = sb("bo", [P, D])
        wp_raw = sb("wp_raw", [P, D])
        sim_raw = sb("sim_raw", [E, D])
        sim_sq = sb("sim_sq", [E, D])
        sim_n = sb("sim_n", [E, D])
        sim_s = sb("sim_s", [E, 4])
        inv_temp = sb("inv_temp", [E, 1])
        simT = sb("simT", [P, E])
        GW = D + E
        gate_hi, gate_lo = sb("gate_hi", [P, GW], F32R), sb("gate_lo", [P, GW], F32R)
        b1_rows, b1_col = sb("b1_rows", [SLOTS, P]), sb("b1_col", [P, SLOTS])
        b2_rows, b2_col = sb("b2_rows", [E, D]), sb("b2_col", [P, E])
        w1_hi, w1_lo = sb("w1_hi", [P, E * F], F32R), sb("w1_lo", [P, E * F], F32R)
        w2_hi, w2_lo = sb("w2_hi", [P, E * F], F32R), sb("w2_lo", [P, E * F], F32R)

        x_tok = sb("x_tok", [P, T, D])
        xb = sb("xb", [P, T, D])
        xT_hi, xT_lo = sb("xT_hi", [P, N], F32R), sb("xT_lo", [P, N], F32R)
        v_ext = sb("v_ext", [P, T, HEADS, VW])
        expo = sb("expo", [P, 2, 2 * NF])
        k_feat = sb("k_feat", [P, T, NF])
        q_feat = sb("q_feat", [P, FC, N])
        kv_bd = sb("kv_bd", [P, FC, HC, VW])
        den = sb("den", [P, T, HEADS])
        inv_den = sb("inv_den", [P, T, HEADS])
        attn = sb("attn", [P, T, HEADS, HD])
        attnT = sb("attnT", [P, N])
        s1 = sb("s1", [P, T, D])
        st1, mv1 = sb("st1", [P, T, 6]), sb("mv1", [P, T, 2])
        ve1, rs1 = sb("ve1", [P, T]), sb("rs1", [P, T])
        x2 = sb("x2", [P, T, D])

        squares = sb("squares", [P, T, D])
        norm_sq, norm_c, inv_norm = sb("norm_sq", [P, T]), sb("norm_c", [P, T]), sb("inv_norm", [P, T])
        scores = sb("scores", [P, T, E])
        best = sb("best", [P, T, TOP])
        best_i = sb("best_i", [P, T, TOP], U32)
        gap, gap_tanh = sb("gap", [P, T]), sb("gap_tanh", [P, T])
        probs = sb("probs", [P, T, 2])
        chosen = sb("chosen", [P, T, 2, E])
        weighted = sb("weighted", [P, T, 2, E])
        comb = sb("comb", [P, T, E])
        combT = sb("combT", [E, N])
        comb_wide = sb("comb_wide", [P, E, N])

        x2T_hi, x2T_lo = sb("x2T_hi", [P, N], F32R), sb("x2T_lo", [P, N], F32R)
        h = sb("h", [P, RING, 2 * N])
        h_hi, h_lo = sb("h_hi", [P, RING, 2 * N], F32R), sb("h_lo", [P, RING, 2 * N], F32R)
        scaled = sb("scaled", [P, 2, N])
        yT = sb("yT", [P, N])
        st2, mv2 = sb("st2", [P, T, 6]), sb("mv2", [P, T, 2])
        ve2, rs2 = sb("ve2", [P, T]), sb("rs2", [P, T])
        y_out = sb("y_out", [P, T, D])
        proj_bd = y_out[:, :, :].rearrange("p t d -> p (t d)").rearrange("p (h f) -> p h f", h=HEADS)
        w1_raw = h[:, :, :].rearrange("p r n -> p (r n)")
        w2_raw = comb_wide[:, :, :].rearrange("p e n -> p (e n)")

        up_ps = [ctx.enter_context(nc.psum_tensor(f"up_ps{i}", [P, N], F32)) for i in range(UPB)]
        down_ps = [ctx.enter_context(nc.psum_tensor(f"down_ps{i}", [P, N], F32)) for i in range(2)]
        pair = [ctx.enter_context(nc.psum_tensor(f"att_ps{i}", [P, 2, N], F32)) for i in range(2)]
        A = [pair[0][:, 0, :], pair[0][:, 1, :], pair[1][:, 0, :], pair[1][:, 1, :]]

        s_in_qkv, s_in_wo, s_in_gate, s_in_bias, s_in_w1, s_in_w2 = (
            sem("s_in_" + n) for n in ("qkv", "wo", "gate", "bias", "w1", "w2"))
        s_const = sem("s_const")
        s_proj_bd = sem("s_proj_bd")
        s_wqkT_ps, s_wqkT = sem("s_wqkT_ps"), sem("s_wqkT")
        s_fold, s_fold_hi, s_fold_lo = sem("s_fold"), sem("s_fold_hi"), sem("s_fold_lo")
        s_sim, s_sim_root = sem("s_sim"), sem("s_sim_root")
        s_cols_ps, s_cols = sem("s_cols_ps"), sem("s_cols")
        s_gfold, s_gw_hi, s_gw_lo = sem("s_gfold"), sem("s_gw_hi"), sem("s_gw_lo")
        s_w1_hi, s_w1_lo, s_w2_hi, s_w2_lo = sem("s_w1_hi"), sem("s_w1_lo"), sem("s_w2_hi"), sem("s_w2_lo")

        s_x_in = sem("s_x_in")
        s_xb = sem("s_xb")
        s_xT, s_xT_hi, s_xT_lo = sem("s_xT"), sem("s_xT_hi"), sem("s_xT_lo")
        s_v, s_v_ext = sem("s_v"), sem("s_v_ext")
        s_pre = sem("s_pre")
        s_exp, s_cap, s_feat = sem("s_exp"), sem("s_cap"), sem("s_feat")
        s_kv, s_kv_bd = sem("s_kv"), sem("s_kv_bd")
        s_num, s_den, s_attn = sem("s_num"), sem("s_den"), sem("s_attn")
        s_aT, s_attnT = sem("s_aT"), sem("s_attnT")
        s_mix = sem("s_mix")
        s_ln1 = sem("s_ln1")
        s_rs1, s_x2 = sem("s_rs1"), sem("s_x2")
        s_x2T, s_x2T_hi, s_x2T_lo = sem("s_x2T"), sem("s_x2T_hi"), sem("s_x2T_lo")
        s_gate, s_sq = sem("s_gate"), sem("s_sq")
        s_nc, s_in_norm = sem("s_nc"), sem("s_in_norm")
        s_scores = sem("s_scores")
        s_best, s_gap, s_tanh = sem("s_best"), sem("s_gap"), sem("s_tanh")
        s_route, s_comb = sem("s_route"), sem("s_comb")
        s_combT, s_combT_sb, s_combT_out = sem("s_combT"), sem("s_combT_sb"), sem("s_combT_out")
        s_wide = [sem(f"s_wide{e}") for e in range(E)]
        s_up, s_gelu = sem("s_up"), sem("s_gelu")
        s_hi_act, s_hi_dve = sem("s_hi_act"), sem("s_hi_dve")
        s_lo, s_used = sem("s_lo"), sem("s_used")
        s_scaled = sem("s_scaled")
        s_added = sem("s_added")
        s_yT = sem("s_yT")
        s_ln2 = sem("s_ln2")
        s_rs2, s_y, s_out = sem("s_rs2"), sem("s_y"), sem("s_out")

        HI_ACT, HI_DVE = UNITS - len(HI_ON_DVE), len(HI_ON_DVE)
        hi_rank = [sum((v in HI_ON_DVE) == (u in HI_ON_DVE) for v in range(u + 1)) for u in range(UNITS)]

        x_view = x.rearrange("s (p t) d -> s p t d", t=T)
        out_view = out.rearrange("s (p t) d -> s p t d", t=T)

        def cols(t):
            return slice(t * P, (t + 1) * P)

        def half(i):
            return slice(i * N, (i + 1) * N)

        def wait_if(eng, semaphore, value):
            if isinstance(value, int) and value <= 0:
                return
            eng.wait_ge(semaphore, value)

        def wait_apart(eng, semaphore, value):
            if isinstance(value, int):
                wait_if(eng, semaphore, value)
                return
            value = eng.to_reg(value)
            eng.wait_ge(s_const, 12)
            eng.wait_ge(semaphore, value)

        block = ctx.enter_context(nc.Block())

        @block.sync
        def _(sp):
            def load_x(b):
                wait_apart(sp, s_xT, b)
                wait_apart(sp, s_xb, b)
                sp.dma_start(x_tok[:, :, :], x_view[b]).then_inc(s_x_in, 16)

            def spread_comb(b):
                wait_apart(sp, s_combT_sb, b + 1)
                for e in range(E):
                    wait_apart(sp, s_wide[e], 16 * b)
                sp.dma_start(comb_dram, combT[:, :]).then_inc(s_combT_out, 16)
                wait_apart(sp, s_combT_out, 16 * b + 16)
                for e in range(E):
                    wait_apart(sp, s_scaled, E * (b - 1) + e + 1)
                    sp.dma_start(comb_wide[:, e, :], comb_dram[e, :].partition_broadcast(P)).then_inc(s_wide[e], 16)

            def store(b):
                wait_apart(sp, s_y, b + 1)
                sp.dma_start(out_view[b], y_out[:, :, :]).then_inc(s_out, 16)

            sp.dma_start(wqkv_raw[:, :], w_qkv).then_inc(s_in_qkv, 16)
            sp.dma_start(proj_raw[:, :], proj_matrix.rearrange("h i f -> (h i) f")).then_inc(s_in_qkv, 16)
            load_x(0)
            sp.dma_start(wo[:, :], w_out).then_inc(s_in_wo, 16)
            sp.dma_start(bo[:, :], b_out.partition_broadcast(P)).then_inc(s_in_wo, 16)
            sp.dma_start(wp_raw[:, :], wp).then_inc(s_in_gate, 16)
            sp.dma_start(sim_raw[:, :], sim).then_inc(s_in_gate, 16)
            sp.dma_start(sim_s[:, 0:1], temperature.partition_broadcast(E)).then_inc(s_in_gate, 16)
            sp.dma_start(b1_rows[:, :], b1.rearrange("e (c p) -> (e c) p", p=P)).then_inc(s_in_bias, 16)
            sp.dma_start(b2_rows[:, :], b2).then_inc(s_in_bias, 16)
            sp.dma_start(w1_raw.rearrange("p (e f) -> p e f", e=E), w1.rearrange("e d f -> d e f"))\
                .then_inc(s_in_w1, 16)
            sp.dma_start(w2_raw.rearrange("p (e c d) -> p e c d", e=E, c=CH),
                         w2.rearrange("e (c p) d -> p e c d", p=P)).then_inc(s_in_w2, 16)
            load_x(1)
            sp.wait_ge(s_w2_lo, 1)
            spread_comb(0)
            load_x(2)
            store(0)
            with sp.Fori(1, SEQS - 2) as b:
                spread_comb(b)
                load_x(b + 2)
                store(b)
            for b in (SEQS - 2, SEQS - 1):
                spread_comb(b)
                store(b)
            sp.wait_ge(s_out, 16 * SEQS)

        @block.gpsimd
        def _(pool):
            def bias_x(b):
                pool.wait_ge(s_x_in, 16 * b + 16)
                wait_if(pool, s_ln1, 4 * (b - 1) + 1)
                nc.gpsimd.tensor_tensor(xb[:, :, :], x_tok[:, :, :],
                                        bo[:, :].unsqueeze(1).broadcast_to([P, T, D]), ALU.add).then_inc(s_xb, 1)

            def cap(b, i):
                wait_apart(pool, s_exp, 4 * b + i + 1)
                nc.gpsimd.tensor_scalar(expo[:, i % 2, :], expo[:, i % 2, :], 1.0, 0.0, ALU.min, ALU.max)\
                    .then_inc(s_cap, 1)

            def root_ln1(b):
                pool.wait_ge(s_ln1, 4 * b + 4)
                nc.gpsimd.tensor_tensor(rs1[:, :], ve1[:, :], minus_half[:, :], ALU.pow).then_inc(s_rs1, 1)

            def root_norm(b):
                pool.wait_ge(s_nc, b + 1)
                nc.gpsimd.tensor_tensor(inv_norm[:, :], norm_c[:, :], minus_half[:, :], ALU.pow).then_inc(s_in_norm, 1)

            def root_ln2(b):
                pool.wait_ge(s_ln2, 3 * b + 3)
                nc.gpsimd.tensor_tensor(rs2[:, :], ve2[:, :], minus_half[:, :], ALU.pow).then_inc(s_rs2, 1)

            def start_y(b):
                pool.wait_ge(s_x2T_lo, b + 1)
                wait_if(pool, s_yT, b)
                nc.gpsimd.tensor_tensor(yT[:, :], x2T_hi[:, :].bitcast(F32), x2T_lo[:, :].bitcast(F32), ALU.add)\
                    .then_inc(s_added, 1)

            def add_expert(b, e):
                pool.wait_ge(s_scaled, E * b + e + 1)
                pool.wait_ge(s_added, (E + 1) * b + e + 1)
                nc.gpsimd.tensor_tensor(yT[:, :], yT[:, :], scaled[:, e % 2, :], ALU.add).then_inc(s_added, 1)

            nc.gpsimd.memset(ident[:, :], 0.0).then_inc(s_const, 1)
            nc.gpsimd.memset(head_mask[:, :], 1.0).then_inc(s_const, 1)
            nc.gpsimd.memset(kv_mask[:, :], 1.0).then_inc(s_const, 1)
            nc.gpsimd.memset(minus_half[:, :], -0.5).then_inc(s_const, 1)
            nc.gpsimd.iota(iota_i[:, :, :, :], [[0, T], [0, 2], [1, E]], base=0, channel_multiplier=0)\
                .then_inc(s_const, 1)
            pool.wait_ge(s_const, 5)
            nc.gpsimd.affine_select(out=ident[:, :], in_=ident[:, :], compare_op=ALU.not_equal, fill=1.0, base=0,
                                    pattern=[[-1, P]], channel_multiplier=1).then_inc(s_const, 1)
            nc.gpsimd.tensor_copy(iota8[:, :, :, :], iota_i[:, :, :, :]).then_inc(s_const, 1)
            nc.gpsimd.affine_select(out=head_mask[:, :], in_=head_mask[:, :], compare_op=ALU.is_ge, fill=0.0, base=0,
                                    pattern=[[-HD, HEADS]], channel_multiplier=1).then_inc(s_const, 1)
            nc.gpsimd.affine_select(out=kv_mask[:, :], in_=kv_mask[:, :], compare_op=ALU.is_ge, fill=0.0, base=0,
                                    pattern=[[-FEAT, HC]], channel_multiplier=1).then_inc(s_const, 1)
            pool.wait_ge(s_const, 9)
            nc.gpsimd.affine_select(out=head_mask[:, :], in_=head_mask[:, :], compare_op=ALU.is_ge, fill=0.0,
                                    base=HD - 1, pattern=[[HD, HEADS]], channel_multiplier=-1).then_inc(s_const, 1)
            nc.gpsimd.affine_select(out=kv_mask[:, :], in_=kv_mask[:, :], compare_op=ALU.is_ge, fill=0.0,
                                    base=FEAT - 1, pattern=[[FEAT, HC]], channel_multiplier=-1).then_inc(s_const, 1)
            nc.gpsimd.memset(v_ext[:, :, :, :], 1.0).then_inc(s_const, 1)
            pool.wait_ge(s_sim, 3)
            nc.gpsimd.tensor_tensor(sim_s[:, 2:3], sim_s[:, 1:2], minus_half[0:E, 0:1], ALU.pow).then_inc(s_sim_root, 1)
            pool.wait_ge(s_in_wo, 32)
            bias_x(0)
            for i in range(4):
                cap(0, i)
            root_ln1(0)
            root_norm(0)
            start_y(0)

            def step(b):
                cap(b + 1, 0)
                bias_x(b + 1)
                cap(b + 1, 1)
                add_expert(b, 0)
                cap(b + 1, 2)
                add_expert(b, 1)
                cap(b + 1, 3)
                for e in (2, 3, 4):
                    add_expert(b, e)
                root_ln1(b + 1)
                for e in (5, 6, 7):
                    add_expert(b, e)
                root_norm(b + 1)
                root_ln2(b)
                start_y(b + 1)

            step(0)
            with pool.Fori(1, SEQS - 1) as b:
                step(b)
            for e in range(E):
                add_expert(SEQS - 1, e)
            root_ln2(SEQS - 1)

        @block.tensor
        def _(pe):
            def three(dst, w_hi, w_lo, m_hi, m_lo, start=True, stop=True):
                nc.tensor.matmul(dst, w_hi, m_hi, start=start, stop=False)
                nc.tensor.matmul(dst, w_hi, m_lo, start=False, stop=False)
                return nc.tensor.matmul(dst, w_lo, m_hi, start=False, stop=stop)

            def transpose_x(b):
                pe.wait_ge(s_x_in, 16 * b + 16)
                wait_if(pe, s_scores, b)
                for t in range(T):
                    mm = nc.tensor.transpose(A[0][:, cols(t)], x_tok[:, t, :], ident[:, :])
                mm.then_inc(s_xT, 1)

            def values(b):
                pe.wait_ge(s_xT_lo, b + 1)
                wait_if(pe, s_combT_sb, b)
                for t in range(T):
                    mm = three(A[1][:, cols(t)], xT_hi[:, cols(t)], xT_lo[:, cols(t)], wv_hi[:, :], wv_lo[:, :])
                mm.then_inc(s_v, 1)

            def keys(b, i):
                if i == 0:
                    wait_if(pe, s_y, b - 1)
                else:
                    pe.wait_ge(s_v_ext, b + 1)
                for j in range(2):
                    t = cols(2 * i + j)
                    mm = three(pair[1 - i][:, j, :], xT_hi[:, t], xT_lo[:, t], wk_hi[:, :], wk_lo[:, :])
                mm.then_inc(s_pre, 1)

            def queries(b, i):
                pe.wait_ge(s_feat, 4 * b + i + 1)
                for j in range(2):
                    c = cols(2 * i + j)
                    mm = three(pair[1 - i][:, j, :], wq_hi[:, c], wq_lo[:, c], xT_hi[:, :], xT_lo[:, :])
                mm.then_inc(s_pre, 1)

            def sum_keys_values(b):
                pe.wait_ge(s_feat, 4 * b + 3)
                for c in range(FC):
                    for t in range(T):
                        mm = nc.tensor.matmul(A[2][:, c * KC:(c + 1) * KC], k_feat[:, t, cols(c)],
                                              v_ext[:, t, c * HC:(c + 1) * HC, :], start=(t == 0), stop=(t == T - 1))
                mm.then_inc(s_kv, 1)

            def numerators(b):
                pe.wait_ge(s_feat, 4 * b + 4)
                pe.wait_ge(s_kv_bd, b + 1)
                for t in range(T):
                    for c in range(FC):
                        at = (t % 2 * FC + c) * KC
                        mm = nc.tensor.matmul(A[3 if t < 2 else 0][:, at:at + KC], q_feat[:, c, cols(t)],
                                              kv_bd[:, c, :, :], start=True, stop=True)
                mm.then_inc(s_num, 1)

            def transpose_attn(b):
                pe.wait_ge(s_attn, b + 1)
                for t in range(T):
                    mm = nc.tensor.transpose(A[2][:, cols(t)], attn[:, t, :, :].rearrange("p h i -> p (h i)"), ident[:, :])
                mm.then_inc(s_aT, 1)

            def mix_heads(b):
                pe.wait_ge(s_attnT, b + 1)
                for t in range(T):
                    mm = nc.tensor.matmul(A[1][:, cols(t)], attnT[:, cols(t)], wo[:, :], start=True, stop=True)
                mm.then_inc(s_mix, 1)

            def transpose_x2(b):
                pe.wait_ge(s_x2, b + 1)
                for t in range(T):
                    mm = nc.tensor.transpose(A[2][:, cols(t)], x2[:, t, :], ident[:, :])
                mm.then_inc(s_x2T, 1)

            def gate(b):
                pe.wait_ge(s_x2T_lo, b + 1)
                for t in range(T):
                    at = t % 2 * GW
                    mm = three(A[3 if t < 2 else 0][:, at:at + GW], x2T_hi[:, cols(t)], x2T_lo[:, cols(t)],
                               gate_hi[:, :], gate_lo[:, :])
                mm.then_inc(s_gate, 1)

            def transpose_comb(b):
                pe.wait_ge(s_comb, b + 1)
                for t in range(T):
                    mm = nc.tensor.matmul(A[1][0:E, cols(t)], comb[:, t, :], ident[:, :], start=True, stop=True)
                mm.then_inc(s_combT, 1)

            def transpose_y(b):
                pe.wait_ge(s_added, (E + 1) * (b + 1))
                for t in range(T):
                    mm = nc.tensor.transpose(A[2][:, cols(t)], yT[:, cols(t)], ident[:, :])
                mm.then_inc(s_yT, 1)

            def up(b, s):
                wait_if(pe, s_gelu, b * SLOTS + s - UPB + 1)
                three(up_ps[s % UPB][:, :], w1_hi[:, cols(s)], w1_lo[:, cols(s)],
                      x2T_hi[:, :], x2T_lo[:, :]).then_inc(s_up, 1)

            def down(b, s):
                e, c, u = s // CH, s % CH, s // 2
                if s % 2 == 0:
                    pe.wait_ge(s_lo, b * UNITS + u + 1)
                if c == 0:
                    wait_if(pe, s_scaled, b * E + e - 1)
                mm = three(down_ps[e % 2][:, :], w2_hi[:, cols(s)], w2_lo[:, cols(s)],
                           h_hi[:, u % RING, half(s % 2)], h_lo[:, u % RING, half(s % 2)],
                           start=(c == 0), stop=(c == CH - 1))
                if s % 2 == 1:
                    mm.then_inc(s_used, 1)

            def slot(b, s):
                up(b, s)
                if s >= CH:
                    down(b, s - CH)

            pe.wait_ge(s_const, 12)
            pe.wait_ge(s_in_qkv, 32)
            for i in range(2):
                mm = nc.tensor.transpose(up_ps[1][:, cols(i)], wqkv_raw[:, cols(i)], ident[:, :])
            mm.then_inc(s_wqkT_ps, 1)
            transpose_x(0)
            pe.wait_ge(s_wqkT, 1)
            pe.wait_ge(s_proj_bd, 1)
            for i in range(2):
                mm = nc.tensor.matmul(down_ps[i][:, :], wqkT[:, i, :], y_out[:, :, :].rearrange("p t d -> p (t d)"),
                                      start=True, stop=True)
            mm.then_inc(s_fold, 1)
            pe.wait_ge(s_in_gate, 48)
            pe.wait_ge(s_in_bias, 32)
            pe.wait_ge(s_sim, 5)
            nc.tensor.transpose(up_ps[0][:, 0:P], wp_raw[:, :], ident[:, :])
            nc.tensor.matmul(up_ps[0][:, P:P + E], sim_n[:, :], ident[0:E, 0:E], start=True, stop=True)
            nc.tensor.matmul(up_ps[0][:, P + E:P + 2 * E], b2_rows[:, :], ident[0:E, 0:E], start=True, stop=True)
            nc.tensor.matmul(up_ps[0][:, P + 2 * E:P + 2 * E + SLOTS], b1_rows[:, :], ident[0:SLOTS, 0:SLOTS],
                             start=True, stop=True).then_inc(s_cols_ps, 1)
            pe.wait_ge(s_fold_lo, 3)
            values(0)
            keys(0, 0)
            keys(0, 1)
            queries(0, 0)
            queries(0, 1)
            pe.wait_ge(s_cols, 3)
            nc.tensor.matmul(up_ps[1][:, 0:E], wp_raw[:, :], simT[:, :], start=True, stop=True).then_inc(s_gfold, 1)
            sum_keys_values(0)
            numerators(0)
            transpose_attn(0)
            pe.wait_ge(s_in_wo, 32)
            mix_heads(0)
            transpose_x2(0)
            pe.wait_ge(s_gw_lo, 2)
            gate(0)
            pe.wait_ge(s_w1_lo, 1)
            for s in range(HEAD):
                slot(0, s)
            pe.wait_ge(s_w2_lo, 1)

            def step(b):
                for s in range(HEAD, SLOTS):
                    if s == 5:
                        transpose_x(b + 1)
                    if s == 6:
                        transpose_comb(b)
                    if s == 8:
                        values(b + 1)
                        keys(b + 1, 0)
                    if s == 10:
                        keys(b + 1, 1)
                    if s == 13:
                        queries(b + 1, 0)
                    if s == 16:
                        queries(b + 1, 1)
                    if s == 18:
                        sum_keys_values(b + 1)
                    if s == 20:
                        numerators(b + 1)
                    if s == 22:
                        transpose_attn(b + 1)
                    if s == 24:
                        mix_heads(b + 1)
                    slot(b, s)
                transpose_x2(b + 1)
                for s in range(SLOTS - CH, SLOTS):
                    down(b, s)
                gate(b + 1)
                for s in range(HEAD):
                    if s == 2:
                        transpose_y(b)
                    slot(b + 1, s)

            step(0)
            with pe.Fori(1, SEQS - 1) as b:
                step(b)
            for s in range(HEAD, SLOTS):
                if s == 6:
                    transpose_comb(SEQS - 1)
                slot(SEQS - 1, s)
            for s in range(SLOTS - CH, SLOTS):
                down(SEQS - 1, s)
            transpose_y(SEQS - 1)

        @block.scalar
        def _(act):
            def x_high(b):
                act.wait_ge(s_xT, b + 1)
                wait_if(act, s_pre, 4 * b)
                nc.scalar.activation(xT_hi[:, :], A[0], ACT.Copy).then_inc(s_xT_hi, 1)

            def exps(b, i):
                act.wait_ge(s_pre, 4 * b + i + 1)
                wait_if(act, s_feat, 4 * b + i - 1)
                nc.scalar.activation(expo[:, i % 2, :], pair[1 - i % 2][:, :, :].rearrange("p j n -> p (j n)"),
                                     ACT.Exp).then_inc(s_exp, 1)

            def attention_T(b):
                act.wait_ge(s_aT, b + 1)
                wait_if(act, s_mix, b)
                nc.scalar.activation(attnT[:, :], A[2], ACT.Copy).then_inc(s_attnT, 1)

            def x2_high(b):
                act.wait_ge(s_x2T, b + 1)
                wait_if(act, s_up, SLOTS * b)
                wait_if(act, s_added, (E + 1) * (b - 1) + 1)
                nc.scalar.activation(x2T_hi[:, :], A[2], ACT.Copy).then_inc(s_x2T_hi, 1)

            def square_norms(b):
                act.wait_ge(s_gate, b + 1)
                for t in range(T):
                    at = t % 2 * GW
                    ins = nc.scalar.activation(squares[:, t, :], A[3 if t < 2 else 0][:, at:at + D], ACT.Square,
                                               accum_out=norm_sq[:, t:t + 1])
                ins.then_inc(s_sq, 1)

            def gap_to_tanh(b):
                act.wait_ge(s_gap, b + 1)
                nc.scalar.activation(gap_tanh[:, :], gap[:, :], ACT.Tanh, scale=0.5).then_inc(s_tanh, 1)

            def comb_T(b):
                act.wait_ge(s_combT, b + 1)
                wait_if(act, s_combT_out, 16 * b)
                nc.scalar.activation(combT[:, :], A[1][0:E, :], ACT.Copy).then_inc(s_combT_sb, 1)

            def gelu(b, s):
                u = s // 2
                act.wait_ge(s_up, b * SLOTS + s + 1)
                if s % 2 == 0:
                    wait_if(act, s_lo, b * UNITS + u - RING + 1)
                nc.scalar.activation(h[:, u % RING, half(s % 2)], up_ps[s % UPB][:, :], ACT.Gelu,
                                     bias=b1_col[:, s:s + 1]).then_inc(s_gelu, 1)

            def high(b, u):
                if u in HI_ON_DVE:
                    return
                act.wait_ge(s_gelu, b * SLOTS + 2 * u + 2)
                wait_if(act, s_used, b * UNITS + u - RING + 1)
                nc.scalar.activation(h_hi[:, u % RING, :], h[:, u % RING, :], ACT.Copy).then_inc(s_hi_act, 1)

            def slot(b, s):
                gelu(b, s)
                if s % 2 == 0 and s:
                    high(b, s // 2 - 1)

            act.wait_ge(s_wqkT_ps, 1)
            nc.scalar.activation(wqkT[:, :, :].rearrange("p i d -> p (i d)"), up_ps[1][:, 0:2 * P], ACT.Copy)\
                .then_inc(s_wqkT, 1)
            nc.scalar.activation(wv_hi[:, :], wqkv_raw[:, 2 * D:3 * D], ACT.Copy).then_inc(s_fold_hi, 1)
            x_high(0)
            act.wait_ge(s_fold, 1)
            nc.scalar.activation(wk_hi[:, :], down_ps[1][:, :], ACT.Copy).then_inc(s_fold_hi, 1)
            nc.scalar.activation(wq_hi[:, :], down_ps[0][:, :], ACT.Copy).then_inc(s_fold_hi, 1)
            act.wait_ge(s_cols_ps, 1)
            nc.scalar.activation(gate_hi[:, 0:D], up_ps[0][:, 0:D], ACT.Copy).then_inc(s_gw_hi, 1)
            nc.scalar.activation(simT[:, :], up_ps[0][:, P:P + E], ACT.Copy).then_inc(s_cols, 1)
            nc.scalar.activation(b2_col[:, :], up_ps[0][:, P + E:P + 2 * E], ACT.Copy).then_inc(s_cols, 1)
            nc.scalar.activation(b1_col[:, :], up_ps[0][:, P + 2 * E:P + 2 * E + SLOTS], ACT.Copy).then_inc(s_cols, 1)
            exps(0, 0)
            exps(0, 1)
            act.wait_ge(s_in_w1, 16)
            nc.scalar.activation(w1_hi[:, :], w1_raw, ACT.Copy).then_inc(s_w1_hi, 1)
            exps(0, 2)
            exps(0, 3)
            act.wait_ge(s_gfold, 1)
            nc.scalar.activation(gate_hi[:, D:GW], up_ps[1][:, 0:E], ACT.Copy).then_inc(s_gw_hi, 1)
            act.wait_ge(s_in_w2, 16)
            nc.scalar.activation(w2_hi[:, :], w2_raw, ACT.Copy).then_inc(s_w2_hi, 1)
            attention_T(0)
            x2_high(0)
            square_norms(0)
            act.wait_ge(s_w1_lo, 1)
            for s in range(HEAD):
                slot(0, s)
                if s == 2:
                    gap_to_tanh(0)

            def step(b):
                for s in range(HEAD, SLOTS):
                    slot(b, s)
                    if s == 5:
                        x_high(b + 1)
                    if s == 6:
                        comb_T(b)
                    if s == 8:
                        exps(b + 1, 0)
                    if s == 10:
                        exps(b + 1, 1)
                    if s == 13:
                        exps(b + 1, 2)
                    if s == 16:
                        exps(b + 1, 3)
                    if s == 22:
                        attention_T(b + 1)
                high(b, UNITS - 1)
                x2_high(b + 1)
                square_norms(b + 1)
                for s in range(HEAD):
                    slot(b + 1, s)
                gap_to_tanh(b + 1)

            step(0)
            with act.Fori(1, SEQS - 1) as b:
                step(b)
            for s in range(HEAD, SLOTS):
                slot(SEQS - 1, s)
                if s == 6:
                    comb_T(SEQS - 1)
            high(SEQS - 1, UNITS - 1)

        @block.vector
        def _(dve):
            def x_low(b):
                dve.wait_ge(s_xT_hi, b + 1)
                nc.vector.tensor_tensor(xT_lo[:, :], A[0], xT_hi[:, :].bitcast(F32), ALU.subtract).then_inc(s_xT_lo, 1)

            def take_values(b):
                dve.wait_ge(s_v, b + 1)
                wait_if(dve, s_kv, b)
                nc.vector.tensor_copy(v_ext[:, :, :, 0:HD].rearrange("p t h i -> p (t h) i"),
                                      A[1].rearrange("p (g i) -> p g i", i=HD)).then_inc(s_v_ext, 1)

            def features(b, i):
                dve.wait_ge(s_cap, 4 * b + i + 1)
                if i < 2:
                    wait_if(dve, s_kv, b)
                    dst = k_feat[:, 2 * i:2 * i + 2, :]
                else:
                    wait_if(dve, s_num, b)
                    dst = q_feat[:, 2 * i - 4:2 * i - 2, :]
                nc.vector.scalar_tensor_tensor(
                    out=dst.rearrange("p j n -> p (j n)"), in0=pair[1 - i % 2][:, :, :].rearrange("p j n -> p (j n)"),
                    scalar=1.0, in1=expo[:, i % 2, :], op0=ALU.add, op1=ALU.max).then_inc(s_feat, 1)

            def mask_key_values(b):
                dve.wait_ge(s_kv, b + 1)
                wait_if(dve, s_num, b)
                nc.vector.tensor_tensor(kv_bd[:, :, :, :],
                                        A[2][:, 0:FC * KC].rearrange("p (c j i) -> p c j i", c=FC, j=HC),
                                        kv_mask[:, :].unsqueeze(1).unsqueeze(3).broadcast_to([P, FC, HC, VW]),
                                        ALU.mult).then_inc(s_kv_bd, 1)

            def normalize_heads(b):
                dve.wait_ge(s_num, b + 1)
                G = 2 * HEADS
                views = [A[3][:, 0:G * VW].rearrange("p (g i) -> p g i", i=VW),
                         A[0][:, 0:G * VW].rearrange("p (g i) -> p g i", i=VW)]
                flat = den[:, :, :].rearrange("p t h -> p (t h)")
                for i, v in enumerate(views):
                    nc.vector.tensor_scalar(flat[:, i * G:(i + 1) * G], v[:, :, HD], DEN_EPS, None, ALU.add)\
                        .then_inc(s_den, 1)
                dve.wait_ge(s_den, 3 * b + 2)
                nc.vector.reciprocal(inv_den[:, :, :].rearrange("p t h -> p (t h)"), flat).then_inc(s_den, 1)
                dve.wait_ge(s_den, 3 * b + 3)
                wait_if(dve, s_aT, b)
                for i, v in enumerate(views):
                    ins = nc.vector.tensor_tensor(
                        attn[:, 2 * i:2 * i + 2, :, :].rearrange("p t h i -> p (t h) i"), v[:, :, 0:HD],
                        inv_den[:, 2 * i:2 * i + 2, :].rearrange("p t h -> p (t h)").unsqueeze(2)
                        .broadcast_to([P, G, HD]), ALU.mult)
                ins.then_inc(s_attn, 1)

            def row_statistics(rows, stats, moments, biased, semaphore, base):
                for t in range(T):
                    ins = nc.vector.bn_stats(stats[:, t, :], rows(t))
                ins.then_inc(semaphore, 1)
                wait_apart(dve, semaphore, base + 1)
                for t in range(T):
                    ins = nc.vector.bn_aggr(moments[:, t, :], stats[:, t, :])
                ins.then_inc(semaphore, 1)
                dve.wait_ge(semaphore, base + 2)
                nc.vector.tensor_scalar(biased[:, :], moments[:, :, 1], LN_EPS, None, ALU.add).then_inc(semaphore, 1)

            def sum_and_statistics(b):
                dve.wait_ge(s_mix, b + 1)
                dve.wait_ge(s_xb, b + 1)
                nc.vector.tensor_tensor(s1[:, :, :].rearrange("p t d -> p (t d)"), A[1],
                                        xb[:, :, :].rearrange("p t d -> p (t d)"), ALU.add).then_inc(s_ln1, 1)
                dve.wait_ge(s_ln1, 4 * b + 1)
                row_statistics(lambda t: s1[:, t, :], st1, mv1, ve1, s_ln1, 4 * b + 1)

            def norm_rows(b):
                dve.wait_ge(s_rs1, b + 1)
                wait_if(dve, s_x2T, b)
                for t in range(T):
                    ins = nc.vector.tensor_scalar(x2[:, t, :], s1[:, t, :], mv1[:, t, 0:1], rs1[:, t:t + 1],
                                                  ALU.subtract, ALU.mult)
                ins.then_inc(s_x2, 1)

            def x2_low(b):
                dve.wait_ge(s_x2T_hi, b + 1)
                nc.vector.tensor_tensor(x2T_lo[:, :], A[2], x2T_hi[:, :].bitcast(F32), ALU.subtract)\
                    .then_inc(s_x2T_lo, 1)

            def guard_norms(b):
                dve.wait_ge(s_sq, b + 1)
                nc.vector.tensor_scalar(norm_c[:, :], norm_sq[:, :], NORM_EPS ** 2, None, ALU.max).then_inc(s_nc, 1)

            def top_two(b):
                dve.wait_ge(s_in_norm, b + 1)
                for i in range(2):
                    ins = nc.vector.tensor_tensor(
                        scores[:, 2 * i:2 * i + 2, :],
                        A[3 if i == 0 else 0][:, 0:2 * GW].rearrange("p (t g) -> p t g", g=GW)[:, :, D:GW],
                        inv_norm[:, 2 * i:2 * i + 2].unsqueeze(2).broadcast_to([P, 2, E]), ALU.mult)
                ins.then_inc(s_scores, 1)
                wait_apart(dve, s_scores, b + 1)
                for t in range(T):
                    ins = nc.vector.max(best[:, t, :], scores[:, t, :])
                ins.then_inc(s_best, 1)
                dve.wait_ge(s_best, b + 1)
                nc.vector.tensor_tensor(gap[:, :], best[:, :, 0], best[:, :, 1], ALU.subtract).then_inc(s_gap, 1)
                for t in range(T):
                    ins = nc.vector.max_index(best_i[:, t, :], best[:, t, :], scores[:, t, :])
                ins.then_inc(s_route, 1)
                dve.wait_ge(s_route, 3 * b + 1)
                nc.vector.tensor_tensor(chosen[:, :, :, :], iota8[:, :, :, :],
                                        best_i[:, :, 0:2].unsqueeze(3).broadcast_to([P, T, 2, E]), ALU.is_equal)

            def combine(b):
                dve.wait_ge(s_tanh, b + 1)
                nc.vector.tensor_scalar(probs[:, :, 0], gap_tanh[:, :], 0.5, 0.5, ALU.mult, ALU.add)
                nc.vector.tensor_scalar(probs[:, :, 1], gap_tanh[:, :], -0.5, 0.5, ALU.mult, ALU.add)\
                    .then_inc(s_route, 1)
                dve.wait_ge(s_route, 3 * b + 2)
                nc.vector.tensor_tensor(weighted[:, :, :, :], chosen[:, :, :, :],
                                        probs[:, :, :].unsqueeze(3).broadcast_to([P, T, 2, E]), ALU.mult)\
                    .then_inc(s_route, 1)
                dve.wait_ge(s_route, 3 * b + 3)
                wait_if(dve, s_combT, b)
                nc.vector.tensor_tensor(comb[:, :, :], weighted[:, :, 0, :], weighted[:, :, 1, :], ALU.add)\
                    .then_inc(s_comb, 1)

            def low(b, u):
                wait_if(dve, s_used, b * UNITS + u - RING + 1)
                if u in HI_ON_DVE:
                    dve.wait_ge(s_gelu, b * SLOTS + 2 * u + 2)
                    nc.vector.tensor_copy(h_hi[:, u % RING, :], h[:, u % RING, :]).then_inc(s_hi_dve, 1)
                    dve.wait_ge(s_hi_dve, b * HI_DVE + hi_rank[u])
                else:
                    dve.wait_ge(s_hi_act, b * HI_ACT + hi_rank[u])
                nc.vector.tensor_tensor(h_lo[:, u % RING, :], h[:, u % RING, :], h_hi[:, u % RING, :].bitcast(F32),
                                        ALU.subtract).then_inc(s_lo, 1)

            def scale(b, e):
                dve.wait_ge(s_used, b * UNITS + 2 * e + 2)
                dve.wait_ge(s_wide[e], 16 * b + 16)
                wait_if(dve, s_added, (E + 1) * b + (e if e >= 2 else e - 1))
                nc.vector.scalar_tensor_tensor(out=scaled[:, e % 2, :], in0=down_ps[e % 2][:, :],
                                               scalar=b2_col[:, e:e + 1], in1=comb_wide[:, e, :],
                                               op0=ALU.add, op1=ALU.mult).then_inc(s_scaled, 1)

            def last_norm(b):
                dve.wait_ge(s_yT, b + 1)
                row_statistics(lambda t: A[2][:, cols(t)], st2, mv2, ve2, s_ln2, 3 * b)

            def last_rows(b):
                dve.wait_ge(s_rs2, b + 1)
                wait_if(dve, s_out, 16 * b)
                for t in range(T):
                    ins = nc.vector.tensor_scalar(y_out[:, t, :], A[2][:, cols(t)], mv2[:, t, 0:1], rs2[:, t:t + 1],
                                                  ALU.subtract, ALU.mult)
                ins.then_inc(s_y, 1)

            def slot(b, s):
                if s % 2 == 0 and s:
                    low(b, s // 2 - 1)
                if s >= 10 and s % 4 == 2:
                    scale(b, (s - 10) // 4)

            dve.wait_ge(s_const, 12)
            dve.wait_ge(s_in_qkv, 32)
            nc.vector.tensor_tensor(proj_bd, proj_raw[:, :].unsqueeze(1).broadcast_to([P, HEADS, FEAT]),
                                    head_mask[:, :].unsqueeze(2).broadcast_to([P, HEADS, FEAT]), ALU.mult)\
                .then_inc(s_proj_bd, 1)
            dve.wait_ge(s_in_gate, 48)
            nc.vector.tensor_tensor(sim_sq[:, :], sim_raw[:, :], sim_raw[:, :], ALU.mult).then_inc(s_sim, 1)
            dve.wait_ge(s_sim, 1)
            nc.vector.tensor_reduce(sim_s[:, 3:4], sim_sq[:, :], AX.X, ALU.add).then_inc(s_sim, 1)
            dve.wait_ge(s_sim, 2)
            nc.vector.tensor_scalar(sim_s[:, 1:2], sim_s[:, 3:4], NORM_EPS ** 2, None, ALU.max).then_inc(s_sim, 1)
            nc.vector.reciprocal(inv_temp[:, :], sim_s[:, 0:1]).then_inc(s_sim, 1)
            dve.wait_ge(s_sim, 4)
            dve.wait_ge(s_sim_root, 1)
            nc.vector.tensor_scalar(sim_n[:, :], sim_raw[:, :], sim_s[:, 2:3], inv_temp[:, :], ALU.mult, ALU.mult)\
                .then_inc(s_sim, 1)
            x_low(0)
            dve.wait_ge(s_fold_hi, 3)
            for lo, whole, hi in ((wv_lo, wqkv_raw[:, 2 * D:3 * D], wv_hi), (wk_lo, down_ps[1][:, :], wk_hi),
                                  (wq_lo, down_ps[0][:, :], wq_hi)):
                nc.vector.tensor_tensor(lo[:, :], whole, hi[:, :].bitcast(F32), ALU.subtract).then_inc(s_fold_lo, 1)
            take_values(0)
            features(0, 0)
            features(0, 1)
            dve.wait_ge(s_gw_hi, 1)
            dve.wait_ge(s_cols, 3)
            nc.vector.tensor_tensor(gate_lo[:, 0:D], up_ps[0][:, 0:D], gate_hi[:, 0:D].bitcast(F32), ALU.subtract)\
                .then_inc(s_gw_lo, 1)
            features(0, 2)
            features(0, 3)
            dve.wait_ge(s_gw_hi, 2)
            nc.vector.tensor_tensor(gate_lo[:, D:GW], up_ps[1][:, 0:E], gate_hi[:, D:GW].bitcast(F32), ALU.subtract)\
                .then_inc(s_gw_lo, 1)
            mask_key_values(0)
            normalize_heads(0)
            dve.wait_ge(s_w1_hi, 1)
            nc.vector.tensor_tensor(w1_lo[:, :], w1_raw, w1_hi[:, :].bitcast(F32), ALU.subtract).then_inc(s_w1_lo, 1)
            sum_and_statistics(0)
            norm_rows(0)
            x2_low(0)
            dve.wait_ge(s_w2_hi, 1)
            nc.vector.tensor_tensor(w2_lo[:, :], w2_raw, w2_hi[:, :].bitcast(F32), ALU.subtract).then_inc(s_w2_lo, 1)
            guard_norms(0)
            top_two(0)
            for s in range(HEAD):
                slot(0, s)
            combine(0)

            def step(b):
                for s in range(HEAD, SLOTS):
                    slot(b, s)
                    if s == 6:
                        x_low(b + 1)
                    if s == 8:
                        take_values(b + 1)
                    if s == 9:
                        features(b + 1, 0)
                    if s == 11:
                        features(b + 1, 1)
                    if s == 14:
                        features(b + 1, 2)
                    if s == 17:
                        features(b + 1, 3)
                    if s == 18:
                        mask_key_values(b + 1)
                    if s == 20:
                        normalize_heads(b + 1)
                    if s == 24:
                        sum_and_statistics(b + 1)
                    if s == 26:
                        norm_rows(b + 1)
                low(b, UNITS - 1)
                x2_low(b + 1)
                scale(b, E - 2)
                scale(b, E - 1)
                guard_norms(b + 1)
                for s in range(HEAD):
                    if s == 2:
                        top_two(b + 1)
                    slot(b + 1, s)
                last_norm(b)
                combine(b + 1)
                last_rows(b)

            step(0)
            with dve.Fori(1, SEQS - 1) as b:
                step(b)
            for s in range(HEAD, SLOTS):
                slot(SEQS - 1, s)
            low(SEQS - 1, UNITS - 1)
            scale(SEQS - 1, E - 2)
            scale(SEQS - 1, E - 1)
            last_norm(SEQS - 1)
            last_rows(SEQS - 1)


_INS = ["L0_attn_x", "L0_attn_w_qkv", "L0_attn_proj_matrix", "L0_attn_w_out", "L0_attn_b_out", "L0_ffn_Wp",
        "L0_ffn_sim_matrix", "L0_ffn_temperature", "L0_ffn_W1", "L0_ffn_b1", "L0_ffn_W2", "L0_ffn_b2"]


def kernel(**inputs):
    import numpy as _np
    import concourse.bacc as _bacc
    from concourse import mybir as _mybir
    from concourse.bass_utils import run_bass_kernel_spmd as _run

    nc = _bacc.Bacc("TRN2", target_bir_lowering=False, num_devices=1)
    arrays, args = {}, []
    for name in _INS:
        a = _np.ascontiguousarray(inputs[name])
        if a.ndim == 0:
            a = a.reshape(1)
        arrays[f"in_{name}_dram"] = a
        args.append(nc.dram_tensor(f"in_{name}_dram", a.shape, _mybir.dt.from_np(a.dtype), kind="ExternalInput").ap())
    shape = inputs["L0_attn_x"].shape
    out = nc.dram_tensor("out_0_dram", shape, _mybir.dt.float32, kind="ExternalOutput").ap()
    scratch = nc.dram_tensor("comb_scratch", (inputs["L0_ffn_sim_matrix"].shape[0], shape[1]), _mybir.dt.float32,
                             kind="Internal").ap()
    build_layer(nc, *args, out, scratch)
    r = _run(nc, [arrays], core_ids=[0])
    return r.results[0]["out_0_dram"]
```

```python
from contextlib import ExitStack

import concourse.bass as bass
from concourse import mybir

F32 = mybir.dt.float32
F32R = mybir.dt.float32r
U32 = mybir.dt.uint32
ALU = mybir.AluOpType
ACT = mybir.ActivationFunctionType
AX = mybir.AxisListType


def build_layer(nc, x, w_qkv, proj_matrix, w_out, b_out, wp, sim, temperature, w1, b1, w2, b2, out, comb_dram):
    SEQS, N, D = x.shape
    HEADS, HD, FEAT = proj_matrix.shape
    E, _, F = w1.shape
    P = 128
    T = N // P
    NF = HEADS * FEAT
    FC = NF // P
    HC = HEADS // FC
    VW = HD + 1
    KC = HC * VW
    CH = F // P
    SLOTS = E * CH
    UNITS = SLOTS // 2
    RING = 4
    UPB = 2
    TOP = 8
    LN_EPS, DEN_EPS, NORM_EPS = 1e-5, 1e-8, 1e-12
    HEAD = 3
    LAG = 6
    SCALE_LAG = 11
    AHEAD = ((10, 13), (18, 21))
    PE_AT = dict(
        gate=1,
        comb=9, y=7,
        x=3, values=7,
        keys0=9, keys1=9, kv0=16, kv1=17,
        queries0=17, queries1=17, num0=21, num1=24,
        attnT=27, mix=28,
    )
    ACT_AT = dict(
        squares=2,
        tanh=6, comb_T=9, y_copy=8,
        x_high=4, exp_k=9, exp_q=17, attn_copy=26,
    )
    DVE_AT = dict(
        guard=1, last_scale=2,
        top=3, combine=3, y_stats=4, y_rows=12,
        x_low=3, take=4, feat0=9, feat1=11, mask=12,
        feat2=16, feat3=17, heads=23, stats=27, rows=28,
    )
    WARM = (4, 6, 6, 2, 6, 14, 6, 24, 6)
    HI_ON_DVE = (3, 7, 12)
    assert D == P and N == 512 and NF == 512 and UNITS % RING == 0

    with ExitStack() as ctx:
        def sb(name, shape, dt=F32):
            return ctx.enter_context(nc.sbuf_tensor(name, shape, dt))

        def sem(name):
            return ctx.enter_context(nc.semaphore(name))

        ident = sb("ident", [P, P])
        iota8 = sb("iota8", [P, T, 2, E])
        iota_i = sb("iota_i", [P, T, 2, E], mybir.dt.int32)
        head_mask = sb("head_mask", [P, HEADS])
        kv_mask = sb("kv_mask", [P, HC])
        minus_half = sb("minus_half", [P, T])
        table_probe = sb("table_probe", [P, 1])
        wqkv_raw = sb("wqkv_raw", [P, 3 * D])
        proj_raw = sb("proj_raw", [P, FEAT])
        wqkT = sb("wqkT", [P, 2, P])
        wq_hi, wq_lo = sb("wq_hi", [P, NF], F32R), sb("wq_lo", [P, NF], F32R)
        wk_hi, wk_lo = sb("wk_hi", [P, NF], F32R), sb("wk_lo", [P, NF], F32R)
        wv_hi, wv_lo = sb("wv_hi", [P, D], F32R), sb("wv_lo", [P, D], F32R)
        wo = sb("wo", [P, D])
        bo = sb("bo", [P, D])
        wp_raw = sb("wp_raw", [P, D])
        sim_raw = sb("sim_raw", [E, D])
        sim_sq = sb("sim_sq", [E, D])
        sim_n = sb("sim_n", [E, D])
        sim_s = sb("sim_s", [E, 4])
        inv_temp = sb("inv_temp", [E, 1])
        simT = sb("simT", [P, E])
        GW = D + E
        gate_hi, gate_lo = sb("gate_hi", [P, GW], F32R), sb("gate_lo", [P, GW], F32R)
        b1_rows, b1_col = sb("b1_rows", [SLOTS, P]), sb("b1_col", [P, SLOTS])
        b2_rows, b2_col = sb("b2_rows", [E, D]), sb("b2_col", [P, E])
        w1_hi, w1_lo = sb("w1_hi", [P, E * F], F32R), sb("w1_lo", [P, E * F], F32R)
        w2_hi, w2_lo = sb("w2_hi", [P, E * F], F32R), sb("w2_lo", [P, E * F], F32R)

        x_tok = sb("x_tok", [P, T, D])
        xb = sb("xb", [P, T, D])
        xT_hi, xT_lo = sb("xT_hi", [P, N], F32R), sb("xT_lo", [P, N], F32R)
        v_ext = sb("v_ext", [P, T, HEADS, VW])
        expo = sb("expo", [P, 2, 2 * NF])
        k_feat = sb("k_feat", [P, T, NF])
        q_feat = sb("q_feat", [P, FC, N])
        kv_bd = sb("kv_bd", [P, FC, HC, VW])
        den = sb("den", [P, T, HEADS])
        inv_den = sb("inv_den", [P, T, HEADS])
        attn = sb("attn", [P, T, HEADS, HD])
        attnT = sb("attnT", [P, N])
        s1 = sb("s1", [P, T, D])
        st1, mv1 = sb("st1", [P, T, 6]), sb("mv1", [P, T, 2])
        ve1, rs1 = sb("ve1", [P, T]), sb("rs1", [P, T])
        x2 = sb("x2", [P, T, D])

        squares = sb("squares", [P, T, D])
        norm_sq, norm_c, inv_norm = sb("norm_sq", [P, T]), sb("norm_c", [P, T]), sb("inv_norm", [P, T])
        scores = sb("scores", [P, T, E])
        best = sb("best", [P, T, TOP])
        best_i = sb("best_i", [P, T, TOP], U32)
        gap, gap_tanh = sb("gap", [P, T]), sb("gap_tanh", [P, T])
        probs = sb("probs", [P, T, 2])
        chosen = sb("chosen", [P, T, 2, E])
        weighted = sb("weighted", [P, T, 2, E])
        comb = sb("comb", [P, T, E])
        combT = sb("combT", [E, N])
        comb_wide = sb("comb_wide", [P, E, N])

        x2T_hi, x2T_lo = sb("x2T_hi", [P, N], F32R), sb("x2T_lo", [P, N], F32R)
        h = sb("h", [P, RING, 2 * N])
        h_hi, h_lo = sb("h_hi", [P, RING, 2 * N], F32R), sb("h_lo", [P, RING, 2 * N], F32R)
        scaled = sb("scaled", [P, 2, N])
        yT = sb("yT", [P, N])
        st2, mv2 = sb("st2", [P, T, 6]), sb("mv2", [P, T, 2])
        ve2, rs2 = sb("ve2", [P, T]), sb("rs2", [P, T])
        y_out = sb("y_out", [P, T, D])
        proj_bd = y_out[:, :, :].rearrange("p t d -> p (t d)").rearrange("p (h f) -> p h f", h=HEADS)
        w1_raw = h[:, :, :].rearrange("p r n -> p (r n)")
        w2_raw = comb_wide[:, :, :].rearrange("p e n -> p (e n)")

        up_ps = [ctx.enter_context(nc.psum_tensor(f"up_ps{i}", [P, N], F32)) for i in range(UPB)]
        down_ps = [ctx.enter_context(nc.psum_tensor(f"down_ps{i}", [P, N], F32)) for i in range(2)]
        pair = [ctx.enter_context(nc.psum_tensor(f"att_ps{i}", [P, 2, N], F32)) for i in range(2)]
        A = [pair[0][:, 0, :], pair[0][:, 1, :], pair[1][:, 0, :], pair[1][:, 1, :]]

        s_in_qkv, s_in_wo, s_in_gate, s_in_bias, s_in_w1, s_in_w2 = (
            sem("s_in_" + n) for n in ("qkv", "wo", "gate", "bias", "w1", "w2"))
        s_const = sem("s_const")
        s_ones = sem("s_ones")
        s_proj_bd = sem("s_proj_bd")
        s_wqkT_ps, s_wqkT = sem("s_wqkT_ps"), sem("s_wqkT")
        s_fold, s_fold_hi, s_fold_lo = sem("s_fold"), sem("s_fold_hi"), sem("s_fold_lo")
        s_sim, s_sim_root = sem("s_sim"), sem("s_sim_root")
        s_cols_ps, s_cols = sem("s_cols_ps"), sem("s_cols")
        s_gfold, s_gw_hi, s_gw_lo = sem("s_gfold"), sem("s_gw_hi"), sem("s_gw_lo")
        s_w1_hi, s_w1_lo, s_w2_hi, s_w2_lo = sem("s_w1_hi"), sem("s_w1_lo"), sem("s_w2_hi"), sem("s_w2_lo")

        s_x_in = sem("s_x_in")
        s_xb = sem("s_xb")
        s_xT, s_xT_hi, s_xT_lo = sem("s_xT"), sem("s_xT_hi"), sem("s_xT_lo")
        s_v, s_v_ext = sem("s_v"), sem("s_v_ext")
        s_pre = sem("s_pre")
        s_exp, s_cap, s_feat = sem("s_exp"), sem("s_cap"), sem("s_feat")
        s_kv, s_kv_bd = sem("s_kv"), sem("s_kv_bd")
        s_num, s_den, s_attn = sem("s_num"), sem("s_den"), sem("s_attn")
        s_aT, s_attnT = sem("s_aT"), sem("s_attnT")
        s_mix = sem("s_mix")
        s_ln1 = sem("s_ln1")
        s_rs1, s_x2 = sem("s_rs1"), sem("s_x2")
        s_x2T, s_x2T_hi, s_x2T_lo = sem("s_x2T"), sem("s_x2T_hi"), sem("s_x2T_lo")
        s_gate, s_sq = sem("s_gate"), sem("s_sq")
        s_nc, s_in_norm = sem("s_nc"), sem("s_in_norm")
        s_scores = sem("s_scores")
        s_best, s_gap, s_tanh = sem("s_best"), sem("s_gap"), sem("s_tanh")
        s_route, s_comb = sem("s_route"), sem("s_comb")
        s_combT, s_combT_sb, s_combT_out = sem("s_combT"), sem("s_combT_sb"), sem("s_combT_out")
        s_wide = [sem(f"s_wide{e}") for e in range(E)]
        s_up, s_gelu = sem("s_up"), sem("s_gelu")
        s_hi_act, s_hi_dve = sem("s_hi_act"), sem("s_hi_dve")
        s_lo, s_used = sem("s_lo"), sem("s_used")
        s_scaled = sem("s_scaled")
        s_added = sem("s_added")
        s_yT, s_y_copy = sem("s_yT"), sem("s_y_copy")
        s_ln2 = sem("s_ln2")
        s_rs2, s_y, s_out = sem("s_rs2"), sem("s_y"), sem("s_out")

        HI_ACT, HI_DVE = UNITS - len(HI_ON_DVE), len(HI_ON_DVE)
        hi_rank = [sum((v in HI_ON_DVE) == (u in HI_ON_DVE) for v in range(u + 1)) for u in range(UNITS)]

        x_view = x.rearrange("s (p t) d -> s p t d", t=T)
        out_view = out.rearrange("s (p t) d -> s p t d", t=T)

        def kv_bank(b):
            return down_ps[0] if isinstance(b, int) and b == 0 else A[0]

        weight_part = [slice(i * E * F // 2, (i + 1) * E * F // 2) for i in range(2)]

        def cols(t):
            return slice(t * P, (t + 1) * P)

        def half(i):
            return slice(i * N, (i + 1) * N)

        def wait_if(eng, semaphore, value):
            if isinstance(value, int) and value <= 0:
                return
            eng.wait_ge(semaphore, value)

        def wait_apart(eng, semaphore, value):
            if isinstance(value, int):
                wait_if(eng, semaphore, value)
                return
            value = eng.to_reg(value)
            eng.wait_ge(s_const, 11)
            eng.wait_ge(semaphore, value)

        block = ctx.enter_context(nc.Block())

        @block.sync
        def _(sp):
            def load_x(b):
                wait_apart(sp, s_xT, b)
                wait_apart(sp, s_xb, b)
                sp.dma_start(x_tok[:, :, :], x_view[b]).then_inc(s_x_in, 16)

            def spread_comb(b):
                wait_apart(sp, s_combT_sb, b + 1)
                for e in range(E):
                    wait_apart(sp, s_wide[e], 16 * b)
                sp.dma_start(comb_dram, combT[:, :]).then_inc(s_combT_out, 16)
                wait_apart(sp, s_combT_out, 16 * b + 16)
                for e in range(E):
                    wait_apart(sp, s_scaled, E * (b - 1) + e + 1)
                    sp.dma_start(comb_wide[:, e, :], comb_dram[e, :].partition_broadcast(P)).then_inc(s_wide[e], 16)

            def store(b):
                wait_apart(sp, s_y, b + 1)
                sp.dma_start(out_view[b], y_out[:, :, :]).then_inc(s_out, 16)

            sp.dma_start(wqkv_raw[:, :], w_qkv).then_inc(s_in_qkv, 16)
            sp.dma_start(proj_raw[:, :], proj_matrix.rearrange("h i f -> (h i) f")).then_inc(s_in_qkv, 16)
            load_x(0)
            sp.dma_start(wo[:, :], w_out).then_inc(s_in_wo, 16)
            sp.dma_start(bo[:, :], b_out.partition_broadcast(P)).then_inc(s_in_wo, 16)
            sp.dma_start(wp_raw[:, :], wp).then_inc(s_in_gate, 16)
            sp.dma_start(sim_raw[:, :], sim).then_inc(s_in_gate, 16)
            sp.dma_start(sim_s[:, 0:1], temperature.partition_broadcast(E)).then_inc(s_in_gate, 16)
            sp.dma_start(b1_rows[:, :], b1.rearrange("e (c p) -> (e c) p", p=P)).then_inc(s_in_bias, 16)
            sp.dma_start(b2_rows[:, :], b2).then_inc(s_in_bias, 16)
            sp.dma_start(w1_raw.rearrange("p (e f) -> p e f", e=E), w1.rearrange("e d f -> d e f"))\
                .then_inc(s_in_w1, 16)
            sp.dma_start(w2_raw.rearrange("p (e c d) -> p e c d", e=E, c=CH),
                         w2.rearrange("e (c p) d -> p e c d", p=P)).then_inc(s_in_w2, 16)
            load_x(1)
            sp.wait_ge(s_w2_lo, 2)
            spread_comb(0)
            load_x(2)
            with sp.Fori(1, SEQS - 2) as b:
                spread_comb(b)
                store(b - 1)
                wait_apart(sp, s_out, 16 * b)
                load_x(b + 2)
            for b in (SEQS - 2, SEQS - 1):
                spread_comb(b)
                store(b - 1)
            store(SEQS - 1)
            sp.wait_ge(s_out, 16 * SEQS)

        @block.gpsimd
        def _(pool):
            def bias_x(b):
                pool.wait_ge(s_x_in, 16 * b + 16)
                wait_if(pool, s_ln1, 4 * (b - 1) + 1)
                nc.gpsimd.tensor_tensor(xb[:, :, :], x_tok[:, :, :],
                                        bo[:, :].unsqueeze(1).broadcast_to([P, T, D]), ALU.add).then_inc(s_xb, 1)

            def root_ln1(b):
                pool.wait_ge(s_ln1, 4 * b + 4)
                nc.gpsimd.tensor_tensor(rs1[:, :], ve1[:, :], minus_half[:, :], ALU.pow).then_inc(s_rs1, 1)

            def root_norm(b):
                pool.wait_ge(s_nc, b + 1)
                nc.gpsimd.tensor_tensor(inv_norm[:, :], norm_c[:, :], minus_half[:, :], ALU.pow).then_inc(s_in_norm, 1)

            def root_ln2(b):
                pool.wait_ge(s_ln2, 3 * b + 3)
                nc.gpsimd.tensor_tensor(rs2[:, :], ve2[:, :], minus_half[:, :], ALU.pow).then_inc(s_rs2, 1)

            def start_y(b):
                pool.wait_ge(s_x2T_lo, b + 1)
                wait_if(pool, s_yT, b)
                nc.gpsimd.tensor_tensor(yT[:, :], x2T_hi[:, :].bitcast(F32), x2T_lo[:, :].bitcast(F32), ALU.add)\
                    .then_inc(s_added, 1)

            def add_expert(b, e):
                pool.wait_ge(s_scaled, E * b + e + 1)
                pool.wait_ge(s_added, (E + 1) * b + e + 1)
                nc.gpsimd.tensor_tensor(yT[:, :], yT[:, :], scaled[:, e % 2, :], ALU.add).then_inc(s_added, 1)

            nc.gpsimd.memset(ident[:, :], 0.0).then_inc(s_const, 1)
            nc.gpsimd.memset(head_mask[:, :], 1.0).then_inc(s_const, 1)
            nc.gpsimd.memset(kv_mask[:, :], 1.0).then_inc(s_const, 1)
            nc.gpsimd.memset(minus_half[:, :], -0.5).then_inc(s_const, 1)
            nc.gpsimd.iota(iota_i[:, :, :, :], [[0, T], [0, 2], [1, E]], base=0, channel_multiplier=0)\
                .then_inc(s_const, 1)
            pool.wait_ge(s_const, 5)
            nc.gpsimd.affine_select(out=ident[:, :], in_=ident[:, :], compare_op=ALU.not_equal, fill=1.0, base=0,
                                    pattern=[[-1, P]], channel_multiplier=1).then_inc(s_const, 1)
            nc.gpsimd.tensor_copy(iota8[:, :, :, :], iota_i[:, :, :, :]).then_inc(s_const, 1)
            nc.gpsimd.affine_select(out=head_mask[:, :], in_=head_mask[:, :], compare_op=ALU.is_ge, fill=0.0, base=0,
                                    pattern=[[-HD, HEADS]], channel_multiplier=1).then_inc(s_const, 1)
            nc.gpsimd.affine_select(out=kv_mask[:, :], in_=kv_mask[:, :], compare_op=ALU.is_ge, fill=0.0, base=0,
                                    pattern=[[-FEAT, HC]], channel_multiplier=1).then_inc(s_const, 1)
            pool.wait_ge(s_const, 9)
            nc.gpsimd.affine_select(out=head_mask[:, :], in_=head_mask[:, :], compare_op=ALU.is_ge, fill=0.0,
                                    base=HD - 1, pattern=[[HD, HEADS]], channel_multiplier=-1).then_inc(s_const, 1)
            nc.gpsimd.affine_select(out=kv_mask[:, :], in_=kv_mask[:, :], compare_op=ALU.is_ge, fill=0.0,
                                    base=FEAT - 1, pattern=[[FEAT, HC]], channel_multiplier=-1).then_inc(s_const, 1)
            pool.wait_ge(s_sim, 3)
            nc.gpsimd.tensor_tensor(sim_s[:, 2:3], sim_s[:, 1:2], minus_half[0:E, 0:1], ALU.pow).then_inc(s_sim_root, 1)
            pool.wait_ge(s_in_wo, 32)
            bias_x(0)
            for i, part in enumerate(weight_part):
                pool.wait_ge(s_w1_hi, i + 1)
                nc.gpsimd.tensor_tensor(w1_lo[:, part], w1_raw[:, part], w1_hi[:, part].bitcast(F32), ALU.subtract)\
                    .then_inc(s_w1_lo, 1)
            pool.wait_ge(s_w2_hi, 2)
            part = weight_part[1]
            nc.gpsimd.tensor_tensor(w2_lo[:, part], w2_raw[:, part], w2_hi[:, part].bitcast(F32), ALU.subtract)\
                .then_inc(s_w2_lo, 1)
            root_ln1(0)
            root_norm(0)

            def step(b, first=False):
                if not first:
                    root_ln2(b - 1)
                start_y(b)
                bias_x(b + 1)
                for e in (0, 1, 2, 3, 4):
                    add_expert(b, e)
                root_ln1(b + 1)
                for e in (5, 6):
                    add_expert(b, e)
                root_norm(b + 1)
                add_expert(b, 7)

            step(0, first=True)
            with pool.Fori(1, SEQS - 1) as b:
                step(b)
            root_ln2(SEQS - 2)
            start_y(SEQS - 1)
            for e in range(E):
                add_expert(SEQS - 1, e)
            root_ln2(SEQS - 1)

        @block.tensor
        def _(pe):
            def three(dst, w_hi, w_lo, m_hi, m_lo, start=True, stop=True):
                nc.tensor.matmul(dst, w_hi, m_hi, start=start, stop=False)
                nc.tensor.matmul(dst, w_hi, m_lo, start=False, stop=False)
                return nc.tensor.matmul(dst, w_lo, m_hi, start=False, stop=stop)

            def transpose_x(b):
                pe.wait_ge(s_x_in, 16 * b + 16)
                for t in range(T):
                    mm = nc.tensor.transpose(A[1][:, cols(t)], x_tok[:, t, :], ident[:, :])
                mm.then_inc(s_xT, 1)

            def values(b):
                pe.wait_ge(s_xT_lo, b + 1)
                for t in range(T):
                    mm = three(A[1][:, cols(t)], xT_hi[:, cols(t)], xT_lo[:, cols(t)], wv_hi[:, :], wv_lo[:, :])
                mm.then_inc(s_v, 1)

            def keys(b, i):
                if i == 0:
                    wait_if(pe, s_y_copy, b - 1)
                    wait_if(pe, s_scores, b)
                else:
                    pe.wait_ge(s_v_ext, b + 1)
                    wait_if(pe, s_combT_sb, b)
                for j in range(2):
                    t = cols(2 * i + j)
                    mm = three(pair[1 - i][:, j, :], xT_hi[:, t], xT_lo[:, t], wk_hi[:, :], wk_lo[:, :])
                mm.then_inc(s_pre, 1)

            def queries(b, i):
                pe.wait_ge(s_feat, 4 * b + i + 1)
                if i == 1 and kv_bank(b) is A[0]:
                    pe.wait_ge(s_kv_bd, b + 1)
                for j in range(2):
                    c = cols(2 * i + j)
                    mm = three(pair[1 - i][:, j, :], wq_hi[:, c], wq_lo[:, c], xT_hi[:, :], xT_lo[:, :])
                mm.then_inc(s_pre, 1)

            def sum_keys_values(b, i):
                pe.wait_ge(s_feat, 4 * b + 2)
                bank = kv_bank(b)
                for c in (2 * i, 2 * i + 1):
                    for t in range(T):
                        mm = nc.tensor.matmul(bank[:, c * KC:(c + 1) * KC], k_feat[:, t, cols(c)],
                                              v_ext[:, t, c * HC:(c + 1) * HC, :], start=(t == 0), stop=(t == T - 1))
                if i == 1:
                    mm.then_inc(s_kv, 1)

            def numerators(b, i):
                pe.wait_ge(s_feat, 4 * b + 4)
                pe.wait_ge(s_kv_bd, b + 1)
                for t in (2 * i, 2 * i + 1):
                    for c in range(FC):
                        at = (t % 2 * FC + c) * KC
                        mm = nc.tensor.matmul(A[3 if t < 2 else 0][:, at:at + KC], q_feat[:, c, cols(t)],
                                              kv_bd[:, c, :, :], start=True, stop=True)
                if i == 1:
                    mm.then_inc(s_num, 1)

            def transpose_attn(b):
                pe.wait_ge(s_attn, b + 1)
                for t in range(T):
                    mm = nc.tensor.transpose(A[2][:, cols(t)], attn[:, t, :, :].rearrange("p h i -> p (h i)"),
                                             ident[:, :])
                mm.then_inc(s_aT, 1)

            def mix_heads(b):
                pe.wait_ge(s_attnT, b + 1)
                for t in range(T):
                    mm = nc.tensor.matmul(A[1][:, cols(t)], attnT[:, cols(t)], wo[:, :], start=True, stop=True)
                mm.then_inc(s_mix, 1)

            def transpose_x2(b):
                pe.wait_ge(s_x2, b + 1)
                for t in range(T):
                    mm = nc.tensor.transpose(A[2][:, cols(t)], x2[:, t, :], ident[:, :])
                mm.then_inc(s_x2T, 1)

            def gate(b):
                pe.wait_ge(s_x2T_lo, b + 1)
                for t in range(T):
                    at = t % 2 * GW
                    mm = three(A[3 if t < 2 else 0][:, at:at + GW], x2T_hi[:, cols(t)], x2T_lo[:, cols(t)],
                               gate_hi[:, :], gate_lo[:, :])
                mm.then_inc(s_gate, 1)

            def transpose_comb(b):
                pe.wait_ge(s_comb, b + 1)
                for t in range(T):
                    mm = nc.tensor.transpose(A[0][0:E, cols(t)], comb[:, t, :], ident[:, :])
                mm.then_inc(s_combT, 1)

            def transpose_y(b):
                pe.wait_ge(s_added, (E + 1) * (b + 1))
                for t in range(T):
                    mm = nc.tensor.transpose(A[2][:, cols(t)], yT[:, cols(t)], ident[:, :])
                mm.then_inc(s_yT, 1)

            def up(b, s):
                if s == 0:
                    pe.wait_ge(s_x2T_lo, b + 1)
                wait_if(pe, s_gelu, b * SLOTS + s - UPB + 1)
                three(up_ps[s % UPB][:, :], w1_hi[:, cols(s)], w1_lo[:, cols(s)],
                      x2T_hi[:, :], x2T_lo[:, :]).then_inc(s_up, 1)

            def down(b, s):
                e, c, u = s // CH, s % CH, s // 2
                if s % 2 == 0:
                    pe.wait_ge(s_lo, b * UNITS + u + 1)
                if c == 0:
                    wait_if(pe, s_scaled, b * E + e - 1)
                mm = three(down_ps[e % 2][:, :], w2_hi[:, cols(s)], w2_lo[:, cols(s)],
                           h_hi[:, u % RING, half(s % 2)], h_lo[:, u % RING, half(s % 2)],
                           start=(c == 0), stop=(c == CH - 1))
                if s % 2 == 1:
                    mm.then_inc(s_used, 1)

            def downs_by(s):
                return max(s + 1 - LAG, 0) + sum(first <= s < last for first, last in AHEAD)

            def slot(b, s):
                up(b, s)
                for d in range(downs_by(s - 1), downs_by(s)):
                    down(b, d)

            def keep_warm(n, bank):
                for _ in range(n):
                    nc.tensor.transpose(bank[:, 0:P], ident[:, :], ident[:, :])

            pe.wait_ge(s_const, 11)
            keep_warm(WARM[0], down_ps[1])
            pe.wait_ge(s_in_qkv, 32)
            for i in range(2):
                mm = nc.tensor.transpose(up_ps[1][:, cols(i)], wqkv_raw[:, cols(i)], ident[:, :])
            mm.then_inc(s_wqkT_ps, 1)
            transpose_x(0)
            pe.wait_ge(s_wqkT, 1)
            pe.wait_ge(s_proj_bd, 1)
            for i in (1, 0):
                nc.tensor.matmul(down_ps[i][:, :], wqkT[:, i, :], y_out[:, :, :].rearrange("p t d -> p (t d)"),
                                 start=True, stop=True).then_inc(s_fold, 1)
            pe.wait_ge(s_fold_lo, 1)
            values(0)
            keep_warm(WARM[1], up_ps[1])
            pe.wait_ge(s_fold_lo, 2)
            keys(0, 0)
            keys(0, 1)
            pe.wait_ge(s_in_gate, 48)
            pe.wait_ge(s_in_bias, 32)
            pe.wait_ge(s_sim, 5)
            nc.tensor.transpose(up_ps[0][:, 0:P], wp_raw[:, :], ident[:, :])
            nc.tensor.matmul(up_ps[0][:, P:P + E], sim_n[:, :], ident[0:E, 0:E], start=True, stop=True)
            nc.tensor.matmul(up_ps[0][:, P + E:P + 2 * E], b2_rows[:, :], ident[0:E, 0:E], start=True, stop=True)
            nc.tensor.matmul(up_ps[0][:, P + 2 * E:P + 2 * E + SLOTS], b1_rows[:, :], ident[0:SLOTS, 0:SLOTS],
                             start=True, stop=True).then_inc(s_cols_ps, 1)
            keep_warm(WARM[2], up_ps[1])
            pe.wait_ge(s_fold_lo, 3)
            queries(0, 0)
            keep_warm(WARM[3], down_ps[1])
            queries(0, 1)
            sum_keys_values(0, 0)
            sum_keys_values(0, 1)
            pe.wait_ge(s_cols, 3)
            nc.tensor.matmul(up_ps[1][:, 0:E], wp_raw[:, :], simT[:, :], start=True, stop=True).then_inc(s_gfold, 1)
            keep_warm(WARM[4], down_ps[1])
            numerators(0, 0)
            numerators(0, 1)
            keep_warm(WARM[5], down_ps[1])
            transpose_attn(0)
            keep_warm(WARM[6], down_ps[1])
            pe.wait_ge(s_in_wo, 32)
            mix_heads(0)
            keep_warm(WARM[7], down_ps[1])
            transpose_x2(0)
            keep_warm(WARM[8], down_ps[1])
            pe.wait_ge(s_gw_lo, 2)
            gate(0)
            pe.wait_ge(s_w1_lo, 2)
            for s in range(HEAD):
                slot(0, s)
            pe.wait_ge(s_w2_lo, 2)

            def step(b, first=False):
                for s in range(HEAD, SLOTS):
                    if s == PE_AT["x"]:
                        transpose_x(b + 1)
                    if s == PE_AT["y"] and not first:
                        transpose_y(b - 1)
                    if s == PE_AT["values"]:
                        values(b + 1)
                    if s == PE_AT["comb"]:
                        transpose_comb(b)
                    if s == PE_AT["keys0"]:
                        keys(b + 1, 0)
                    if s == PE_AT["keys1"]:
                        keys(b + 1, 1)
                    if s == PE_AT["kv0"]:
                        sum_keys_values(b + 1, 0)
                    if s == PE_AT["kv1"]:
                        sum_keys_values(b + 1, 1)
                    if s == PE_AT["queries0"]:
                        queries(b + 1, 0)
                    if s == PE_AT["queries1"]:
                        queries(b + 1, 1)
                    if s == PE_AT["num0"]:
                        numerators(b + 1, 0)
                    if s == PE_AT["num1"]:
                        numerators(b + 1, 1)
                    if s == PE_AT["attnT"]:
                        transpose_attn(b + 1)
                    if s == PE_AT["mix"]:
                        mix_heads(b + 1)
                    slot(b, s)
                transpose_x2(b + 1)
                for s in range(SLOTS - LAG, SLOTS - HEAD):
                    down(b, s)
                for s in range(HEAD):
                    slot(b + 1, s)
                    down(b, SLOTS - HEAD + s)
                    if s == PE_AT["gate"]:
                        gate(b + 1)

            step(0, first=True)
            with pe.Fori(1, SEQS - 1) as b:
                step(b)
            for s in range(HEAD, SLOTS):
                if s == PE_AT["y"]:
                    transpose_y(SEQS - 2)
                if s == PE_AT["comb"]:
                    transpose_comb(SEQS - 1)
                slot(SEQS - 1, s)
            for s in range(SLOTS - LAG, SLOTS):
                down(SEQS - 1, s)
            transpose_y(SEQS - 1)

        @block.scalar
        def _(act):
            def load_table(function):
                nc.scalar.activation(table_probe[:, :], minus_half[:, 0:1], function)

            def x_high(b):
                act.wait_ge(s_xT, b + 1)
                wait_if(act, s_pre, 4 * b)
                nc.scalar.activation(xT_hi[:, :], A[1], ACT.Copy).then_inc(s_xT_hi, 1)

            def exps(b, i):
                act.wait_ge(s_pre, 4 * b + i + 1)
                wait_if(act, s_feat, 4 * b + i - 1)
                nc.scalar.activation(expo[:, i % 2, :], pair[1 - i % 2][:, :, :].rearrange("p j n -> p (j n)"),
                                     ACT.Exp).then_inc(s_exp, 1)

            def attention_T(b):
                act.wait_ge(s_aT, b + 1)
                wait_if(act, s_mix, b)
                nc.scalar.activation(attnT[:, :], A[2], ACT.Copy).then_inc(s_attnT, 1)

            def x2_high(b):
                act.wait_ge(s_x2T, b + 1)
                wait_if(act, s_up, SLOTS * b)
                wait_if(act, s_added, (E + 1) * (b - 1) + 1)
                nc.scalar.activation(x2T_hi[:, :], A[2], ACT.Copy).then_inc(s_x2T_hi, 1)

            def square_norms(b):
                act.wait_ge(s_gate, b + 1)
                for t in range(T):
                    at = t % 2 * GW
                    ins = nc.scalar.activation(squares[:, t, :], A[3 if t < 2 else 0][:, at:at + D], ACT.Square,
                                               accum_out=norm_sq[:, t:t + 1])
                ins.then_inc(s_sq, 1)

            def gap_to_tanh(b):
                act.wait_ge(s_gap, b + 1)
                nc.scalar.activation(gap_tanh[:, :], gap[:, :], ACT.Tanh, scale=0.5).then_inc(s_tanh, 1)

            def comb_T(b):
                act.wait_ge(s_combT, b + 1)
                wait_if(act, s_combT_out, 16 * b)
                nc.scalar.activation(combT[:, :], A[0][0:E, :], ACT.Copy).then_inc(s_combT_sb, 1)

            def copy_y(b):
                act.wait_ge(s_yT, b + 1)
                if isinstance(b, int):
                    wait_if(act, s_out, 16 * b)
                else:
                    act.wait_ge(s_x_in, 16 * (b + 3))
                nc.scalar.activation(y_out[:, :, :].rearrange("p t d -> p (t d)"), A[2], ACT.Copy)\
                    .then_inc(s_y_copy, 1)

            def gelu(b, s):
                u = s // 2
                act.wait_ge(s_up, b * SLOTS + s + 1)
                if s % 2 == 0:
                    wait_if(act, s_lo, b * UNITS + u - RING + 1)
                nc.scalar.activation(h[:, u % RING, half(s % 2)], up_ps[s % UPB][:, :], ACT.Gelu,
                                     bias=b1_col[:, s:s + 1]).then_inc(s_gelu, 1)

            def high(b, u):
                if u in HI_ON_DVE:
                    return
                act.wait_ge(s_gelu, b * SLOTS + 2 * u + 2)
                wait_if(act, s_used, b * UNITS + u - RING + 1)
                nc.scalar.activation(h_hi[:, u % RING, :], h[:, u % RING, :], ACT.Copy).then_inc(s_hi_act, 1)

            def slot(b, s):
                gelu(b, s)
                if s % 2 == 0 and s:
                    high(b, s // 2 - 1)

            act.wait_ge(s_const, 11)
            load_table(ACT.Exp)
            act.wait_ge(s_wqkT_ps, 1)
            nc.scalar.activation(wqkT[:, :, :].rearrange("p i d -> p (i d)"), up_ps[1][:, 0:2 * P], ACT.Copy)\
                .then_inc(s_wqkT, 1)
            nc.scalar.activation(wv_hi[:, :], wqkv_raw[:, 2 * D:3 * D], ACT.Copy).then_inc(s_fold_hi, 1)
            x_high(0)
            act.wait_ge(s_fold, 1)
            nc.scalar.activation(wk_hi[:, :], down_ps[1][:, :], ACT.Copy).then_inc(s_fold_hi, 1)
            act.wait_ge(s_fold, 2)
            nc.scalar.activation(wq_hi[:, :], down_ps[0][:, :], ACT.Copy).then_inc(s_fold_hi, 1)
            exps(0, 0)
            exps(0, 1)
            act.wait_ge(s_cols_ps, 1)
            nc.scalar.activation(gate_hi[:, 0:D], up_ps[0][:, 0:D], ACT.Copy).then_inc(s_gw_hi, 1)
            nc.scalar.activation(simT[:, :], up_ps[0][:, P:P + E], ACT.Copy).then_inc(s_cols, 1)
            nc.scalar.activation(b2_col[:, :], up_ps[0][:, P + E:P + 2 * E], ACT.Copy).then_inc(s_cols, 1)
            nc.scalar.activation(b1_col[:, :], up_ps[0][:, P + 2 * E:P + 2 * E + SLOTS], ACT.Copy).then_inc(s_cols, 1)
            act.wait_ge(s_in_w1, 16)
            part = weight_part[0]
            nc.scalar.activation(w1_hi[:, part], w1_raw[:, part], ACT.Copy).then_inc(s_w1_hi, 1)
            exps(0, 2)
            exps(0, 3)
            part = weight_part[1]
            nc.scalar.activation(w1_hi[:, part], w1_raw[:, part], ACT.Copy).then_inc(s_w1_hi, 1)
            act.wait_ge(s_gfold, 1)
            nc.scalar.activation(gate_hi[:, D:GW], up_ps[1][:, 0:E], ACT.Copy).then_inc(s_gw_hi, 1)
            act.wait_ge(s_in_w2, 16)
            for part in weight_part:
                nc.scalar.activation(w2_hi[:, part], w2_raw[:, part], ACT.Copy).then_inc(s_w2_hi, 1)
            load_table(ACT.Gelu)
            attention_T(0)
            x2_high(0)
            square_norms(0)
            act.wait_ge(s_w1_lo, 2)
            for s in range(HEAD):
                slot(0, s)

            def step(b, first=False):
                for s in range(HEAD, SLOTS):
                    if s == ACT_AT["y_copy"] and not first:
                        copy_y(b - 1)
                    if s == ACT_AT["x_high"]:
                        x_high(b + 1)
                    if s == ACT_AT["tanh"]:
                        gap_to_tanh(b)
                    if s == ACT_AT["comb_T"]:
                        comb_T(b)
                    if s == ACT_AT["exp_k"]:
                        load_table(ACT.Exp)
                        exps(b + 1, 0)
                        exps(b + 1, 1)
                    if s == ACT_AT["exp_q"]:
                        load_table(ACT.Exp)
                        exps(b + 1, 2)
                        exps(b + 1, 3)
                    if s == ACT_AT["attn_copy"]:
                        attention_T(b + 1)
                    slot(b, s)
                x2_high(b + 1)
                high(b, UNITS - 1)
                for s in range(HEAD):
                    if s == ACT_AT["squares"]:
                        square_norms(b + 1)
                    slot(b + 1, s)

            step(0, first=True)
            with act.Fori(1, SEQS - 1) as b:
                step(b)
            for s in range(HEAD, SLOTS):
                if s == ACT_AT["tanh"]:
                    gap_to_tanh(SEQS - 1)
                if s == ACT_AT["comb_T"]:
                    comb_T(SEQS - 1)
                if s == ACT_AT["y_copy"]:
                    copy_y(SEQS - 2)
                slot(SEQS - 1, s)
            high(SEQS - 1, UNITS - 1)
            copy_y(SEQS - 1)

        @block.vector
        def _(dve):
            def x_low(b):
                dve.wait_ge(s_xT_hi, b + 1)
                nc.vector.tensor_tensor(xT_lo[:, :], A[1], xT_hi[:, :].bitcast(F32), ALU.subtract).then_inc(s_xT_lo, 1)

            def take_values(b):
                dve.wait_ge(s_ones, 1)
                dve.wait_ge(s_v, b + 1)
                wait_if(dve, s_kv, b)
                nc.vector.tensor_copy(v_ext[:, :, :, 0:HD].rearrange("p t h i -> p (t h) i"),
                                      A[1].rearrange("p (g i) -> p g i", i=HD)).then_inc(s_v_ext, 1)

            def features(b, i):
                dve.wait_ge(s_exp, 4 * b + i + 1)
                nc.vector.tensor_scalar(expo[:, i % 2, :], expo[:, i % 2, :], 1.0, None, ALU.min).then_inc(s_cap, 1)
                dve.wait_ge(s_cap, 4 * b + i + 1)
                if i < 2:
                    wait_if(dve, s_kv, b)
                    dst = k_feat[:, 2 * i:2 * i + 2, :]
                else:
                    wait_if(dve, s_num, b)
                    dst = q_feat[:, 2 * i - 4:2 * i - 2, :]
                nc.vector.scalar_tensor_tensor(
                    out=dst.rearrange("p j n -> p (j n)"), in0=pair[1 - i % 2][:, :, :].rearrange("p j n -> p (j n)"),
                    scalar=1.0, in1=expo[:, i % 2, :], op0=ALU.add, op1=ALU.max).then_inc(s_feat, 1)

            def mask_key_values(b):
                dve.wait_ge(s_kv, b + 1)
                wait_if(dve, s_num, b)
                nc.vector.tensor_tensor(kv_bd[:, :, :, :],
                                        kv_bank(b)[:, 0:FC * KC].rearrange("p (c j i) -> p c j i", c=FC, j=HC),
                                        kv_mask[:, :].unsqueeze(1).unsqueeze(3).broadcast_to([P, FC, HC, VW]),
                                        ALU.mult).then_inc(s_kv_bd, 1)

            def normalize_heads(b):
                dve.wait_ge(s_num, b + 1)
                G = 2 * HEADS
                views = [A[3][:, 0:G * VW].rearrange("p (g i) -> p g i", i=VW),
                         A[0][:, 0:G * VW].rearrange("p (g i) -> p g i", i=VW)]
                flat = den[:, :, :].rearrange("p t h -> p (t h)")
                for i, v in enumerate(views):
                    nc.vector.tensor_scalar(flat[:, i * G:(i + 1) * G], v[:, :, HD], DEN_EPS, None, ALU.add)\
                        .then_inc(s_den, 1)
                dve.wait_ge(s_den, 3 * b + 2)
                nc.vector.reciprocal(inv_den[:, :, :].rearrange("p t h -> p (t h)"), flat).then_inc(s_den, 1)
                dve.wait_ge(s_den, 3 * b + 3)
                wait_if(dve, s_aT, b)
                for i, v in enumerate(views):
                    ins = nc.vector.tensor_tensor(
                        attn[:, 2 * i:2 * i + 2, :, :].rearrange("p t h i -> p (t h) i"), v[:, :, 0:HD],
                        inv_den[:, 2 * i:2 * i + 2, :].rearrange("p t h -> p (t h)").unsqueeze(2)
                        .broadcast_to([P, G, HD]), ALU.mult)
                ins.then_inc(s_attn, 1)

            def row_statistics(rows, stats, moments, biased, semaphore, base):
                for t in range(T):
                    ins = nc.vector.bn_stats(stats[:, t, :], rows(t))
                ins.then_inc(semaphore, 1)
                wait_apart(dve, semaphore, base + 1)
                for t in range(T):
                    ins = nc.vector.bn_aggr(moments[:, t, :], stats[:, t, :])
                ins.then_inc(semaphore, 1)
                dve.wait_ge(semaphore, base + 2)
                nc.vector.tensor_scalar(biased[:, :], moments[:, :, 1], LN_EPS, None, ALU.add).then_inc(semaphore, 1)

            def sum_and_statistics(b):
                dve.wait_ge(s_mix, b + 1)
                dve.wait_ge(s_xb, b + 1)
                nc.vector.tensor_tensor(s1[:, :, :].rearrange("p t d -> p (t d)"), A[1],
                                        xb[:, :, :].rearrange("p t d -> p (t d)"), ALU.add).then_inc(s_ln1, 1)
                dve.wait_ge(s_ln1, 4 * b + 1)
                row_statistics(lambda t: s1[:, t, :], st1, mv1, ve1, s_ln1, 4 * b + 1)

            def norm_rows(b):
                dve.wait_ge(s_rs1, b + 1)
                wait_if(dve, s_x2T, b)
                for t in range(T):
                    ins = nc.vector.tensor_scalar(x2[:, t, :], s1[:, t, :], mv1[:, t, 0:1], rs1[:, t:t + 1],
                                                  ALU.subtract, ALU.mult)
                ins.then_inc(s_x2, 1)

            def x2_low(b):
                dve.wait_ge(s_x2T_hi, b + 1)
                nc.vector.tensor_tensor(x2T_lo[:, :], A[2], x2T_hi[:, :].bitcast(F32), ALU.subtract)\
                    .then_inc(s_x2T_lo, 1)

            def guard_norms(b):
                dve.wait_ge(s_sq, b + 1)
                nc.vector.tensor_scalar(norm_c[:, :], norm_sq[:, :], NORM_EPS ** 2, None, ALU.max).then_inc(s_nc, 1)

            def top_two(b):
                dve.wait_ge(s_in_norm, b + 1)
                for i in range(2):
                    ins = nc.vector.tensor_tensor(
                        scores[:, 2 * i:2 * i + 2, :],
                        A[3 if i == 0 else 0][:, 0:2 * GW].rearrange("p (t g) -> p t g", g=GW)[:, :, D:GW],
                        inv_norm[:, 2 * i:2 * i + 2].unsqueeze(2).broadcast_to([P, 2, E]), ALU.mult)
                ins.then_inc(s_scores, 1)
                wait_apart(dve, s_scores, b + 1)
                for t in range(T):
                    ins = nc.vector.max(best[:, t, :], scores[:, t, :])
                ins.then_inc(s_best, 1)
                dve.wait_ge(s_best, b + 1)
                nc.vector.tensor_tensor(gap[:, :], best[:, :, 0], best[:, :, 1], ALU.subtract).then_inc(s_gap, 1)
                for t in range(T):
                    ins = nc.vector.max_index(best_i[:, t, :], best[:, t, :], scores[:, t, :])
                ins.then_inc(s_route, 1)
                dve.wait_ge(s_route, 3 * b + 1)
                nc.vector.tensor_tensor(chosen[:, :, :, :], iota8[:, :, :, :],
                                        best_i[:, :, 0:2].unsqueeze(3).broadcast_to([P, T, 2, E]), ALU.is_equal)

            def combine(b):
                dve.wait_ge(s_tanh, b + 1)
                nc.vector.tensor_scalar(probs[:, :, 0], gap_tanh[:, :], 0.5, 0.5, ALU.mult, ALU.add)
                nc.vector.tensor_scalar(probs[:, :, 1], gap_tanh[:, :], -0.5, 0.5, ALU.mult, ALU.add)\
                    .then_inc(s_route, 1)
                dve.wait_ge(s_route, 3 * b + 2)
                nc.vector.tensor_tensor(weighted[:, :, :, :], chosen[:, :, :, :],
                                        probs[:, :, :].unsqueeze(3).broadcast_to([P, T, 2, E]), ALU.mult)\
                    .then_inc(s_route, 1)
                dve.wait_ge(s_route, 3 * b + 3)
                wait_if(dve, s_combT, b)
                nc.vector.tensor_tensor(comb[:, :, :], weighted[:, :, 0, :], weighted[:, :, 1, :], ALU.add)\
                    .then_inc(s_comb, 1)

            def low(b, u):
                wait_if(dve, s_used, b * UNITS + u - RING + 1)
                if u in HI_ON_DVE:
                    dve.wait_ge(s_gelu, b * SLOTS + 2 * u + 2)
                    nc.vector.tensor_copy(h_hi[:, u % RING, :], h[:, u % RING, :]).then_inc(s_hi_dve, 1)
                    dve.wait_ge(s_hi_dve, b * HI_DVE + hi_rank[u])
                else:
                    dve.wait_ge(s_hi_act, b * HI_ACT + hi_rank[u])
                nc.vector.tensor_tensor(h_lo[:, u % RING, :], h[:, u % RING, :], h_hi[:, u % RING, :].bitcast(F32),
                                        ALU.subtract).then_inc(s_lo, 1)

            def scale(b, e):
                dve.wait_ge(s_used, b * UNITS + 2 * e + 2)
                dve.wait_ge(s_wide[e], 16 * b + 16)
                wait_if(dve, s_added, (E + 1) * b + (e if e >= 2 else e - 1))
                nc.vector.scalar_tensor_tensor(out=scaled[:, e % 2, :], in0=down_ps[e % 2][:, :],
                                               scalar=b2_col[:, e:e + 1], in1=comb_wide[:, e, :],
                                               op0=ALU.add, op1=ALU.mult).then_inc(s_scaled, 1)

            def last_norm(b):
                dve.wait_ge(s_y_copy, b + 1)
                row_statistics(lambda t: y_out[:, t, :], st2, mv2, ve2, s_ln2, 3 * b)

            def last_rows(b):
                dve.wait_ge(s_rs2, b + 1)
                for t in range(T):
                    ins = nc.vector.tensor_scalar(y_out[:, t, :], y_out[:, t, :], mv2[:, t, 0:1], rs2[:, t:t + 1],
                                                  ALU.subtract, ALU.mult)
                ins.then_inc(s_y, 1)

            def slot(b, s):
                if s % 2 == 0 and s:
                    low(b, s // 2 - 1)
                if s >= SCALE_LAG and (s - SCALE_LAG) % CH == 0:
                    scale(b, (s - SCALE_LAG) // CH)

            nc.vector.memset(v_ext[:, :, :, :], 1.0).then_inc(s_ones, 1)
            dve.wait_ge(s_const, 11)
            dve.wait_ge(s_in_qkv, 32)
            nc.vector.tensor_tensor(proj_bd, proj_raw[:, :].unsqueeze(1).broadcast_to([P, HEADS, FEAT]),
                                    head_mask[:, :].unsqueeze(2).broadcast_to([P, HEADS, FEAT]), ALU.mult)\
                .then_inc(s_proj_bd, 1)
            dve.wait_ge(s_fold_hi, 1)
            nc.vector.tensor_tensor(wv_lo[:, :], wqkv_raw[:, 2 * D:3 * D], wv_hi[:, :].bitcast(F32), ALU.subtract)\
                .then_inc(s_fold_lo, 1)
            x_low(0)
            dve.wait_ge(s_in_gate, 48)
            nc.vector.tensor_tensor(sim_sq[:, :], sim_raw[:, :], sim_raw[:, :], ALU.mult).then_inc(s_sim, 1)
            dve.wait_ge(s_sim, 1)
            nc.vector.tensor_reduce(sim_s[:, 3:4], sim_sq[:, :], AX.X, ALU.add).then_inc(s_sim, 1)
            dve.wait_ge(s_sim, 2)
            nc.vector.tensor_scalar(sim_s[:, 1:2], sim_s[:, 3:4], NORM_EPS ** 2, None, ALU.max).then_inc(s_sim, 1)
            nc.vector.reciprocal(inv_temp[:, :], sim_s[:, 0:1]).then_inc(s_sim, 1)
            dve.wait_ge(s_fold_hi, 2)
            nc.vector.tensor_tensor(wk_lo[:, :], down_ps[1][:, :], wk_hi[:, :].bitcast(F32), ALU.subtract)\
                .then_inc(s_fold_lo, 1)
            take_values(0)
            dve.wait_ge(s_fold_hi, 3)
            nc.vector.tensor_tensor(wq_lo[:, :], down_ps[0][:, :], wq_hi[:, :].bitcast(F32), ALU.subtract)\
                .then_inc(s_fold_lo, 1)
            dve.wait_ge(s_sim, 4)
            dve.wait_ge(s_sim_root, 1)
            nc.vector.tensor_scalar(sim_n[:, :], sim_raw[:, :], sim_s[:, 2:3], inv_temp[:, :], ALU.mult, ALU.mult)\
                .then_inc(s_sim, 1)
            features(0, 0)
            features(0, 1)
            dve.wait_ge(s_gw_hi, 1)
            dve.wait_ge(s_cols, 3)
            nc.vector.tensor_tensor(gate_lo[:, 0:D], up_ps[0][:, 0:D], gate_hi[:, 0:D].bitcast(F32), ALU.subtract)\
                .then_inc(s_gw_lo, 1)
            features(0, 2)
            features(0, 3)
            mask_key_values(0)
            dve.wait_ge(s_gw_hi, 2)
            nc.vector.tensor_tensor(gate_lo[:, D:GW], up_ps[1][:, 0:E], gate_hi[:, D:GW].bitcast(F32), ALU.subtract)\
                .then_inc(s_gw_lo, 1)
            dve.wait_ge(s_w2_hi, 1)
            part = weight_part[0]
            nc.vector.tensor_tensor(w2_lo[:, part], w2_raw[:, part], w2_hi[:, part].bitcast(F32), ALU.subtract)\
                .then_inc(s_w2_lo, 1)
            normalize_heads(0)
            sum_and_statistics(0)
            norm_rows(0)
            x2_low(0)
            guard_norms(0)
            for s in range(HEAD):
                slot(0, s)

            def step(b, first=False):
                for s in range(HEAD, SLOTS):
                    slot(b, s)
                    if s == DVE_AT["top"]:
                        top_two(b)
                    if s == DVE_AT["x_low"]:
                        x_low(b + 1)
                    if s == DVE_AT["y_stats"] and not first:
                        last_norm(b - 1)
                    if s == DVE_AT["y_rows"] and not first:
                        last_rows(b - 1)
                    if s == DVE_AT["combine"]:
                        combine(b)
                    if s == DVE_AT["take"]:
                        take_values(b + 1)
                    if s == DVE_AT["feat0"]:
                        features(b + 1, 0)
                    if s == DVE_AT["feat1"]:
                        features(b + 1, 1)
                    if s == DVE_AT["mask"]:
                        mask_key_values(b + 1)
                    if s == DVE_AT["feat2"]:
                        features(b + 1, 2)
                    if s == DVE_AT["feat3"]:
                        features(b + 1, 3)
                    if s == DVE_AT["heads"]:
                        normalize_heads(b + 1)
                    if s == DVE_AT["stats"]:
                        sum_and_statistics(b + 1)
                    if s == DVE_AT["rows"]:
                        norm_rows(b + 1)
                x2_low(b + 1)
                low(b, UNITS - 1)
                scale(b, E - 2)
                for s in range(HEAD):
                    if s == DVE_AT["last_scale"]:
                        scale(b, E - 1)
                    if s == DVE_AT["guard"]:
                        guard_norms(b + 1)
                    slot(b + 1, s)

            step(0, first=True)
            with dve.Fori(1, SEQS - 1) as b:
                step(b)
            for s in range(HEAD, SLOTS):
                slot(SEQS - 1, s)
                if s == DVE_AT["top"]:
                    top_two(SEQS - 1)
                if s == DVE_AT["y_stats"]:
                    last_norm(SEQS - 2)
                if s == DVE_AT["y_rows"]:
                    last_rows(SEQS - 2)
                if s == DVE_AT["combine"]:
                    combine(SEQS - 1)
            low(SEQS - 1, UNITS - 1)
            scale(SEQS - 1, E - 2)
            scale(SEQS - 1, E - 1)
            last_norm(SEQS - 1)
            last_rows(SEQS - 1)


_INS = ["L0_attn_x", "L0_attn_w_qkv", "L0_attn_proj_matrix", "L0_attn_w_out", "L0_attn_b_out", "L0_ffn_Wp",
        "L0_ffn_sim_matrix", "L0_ffn_temperature", "L0_ffn_W1", "L0_ffn_b1", "L0_ffn_W2", "L0_ffn_b2"]


def kernel(**inputs):
    import numpy as _np
    import concourse.bacc as _bacc
    from concourse import mybir as _mybir
    from concourse.bass_utils import run_bass_kernel_spmd as _run

    nc = _bacc.Bacc("TRN2", target_bir_lowering=False, num_devices=1)
    arrays, args = {}, []
    for name in _INS:
        a = _np.ascontiguousarray(inputs[name])
        if a.ndim == 0:
            a = a.reshape(1)
        arrays[f"in_{name}_dram"] = a
        args.append(nc.dram_tensor(f"in_{name}_dram", a.shape, _mybir.dt.from_np(a.dtype), kind="ExternalInput").ap())
    shape = inputs["L0_attn_x"].shape
    out = nc.dram_tensor("out_0_dram", shape, _mybir.dt.float32, kind="ExternalOutput").ap()
    scratch = nc.dram_tensor("comb_scratch", (inputs["L0_ffn_sim_matrix"].shape[0], shape[1]), _mybir.dt.float32,
                             kind="Internal").ap()
    build_layer(nc, *args, out, scratch)
    r = _run(nc, [arrays], core_ids=[0])
    return r.results[0]["out_0_dram"]
```
